# Optimizing a Trainium2 kernel written in Bass

```python
import numpy as np
import jax
import jax.numpy as jnp

def _softmax(x, axis=-1):
    return jax.nn.softmax(x, axis=axis)

def _gelu(x):
    return jax.nn.gelu(x, approximate=True)

def _silu(x):
    return jax.nn.silu(x)

def _sigmoid(x):
    return jax.nn.sigmoid(x)

def _layernorm(x, axis=-1, eps=1e-05):
    m = jnp.mean(x, axis=axis, keepdims=True)
    v = jnp.var(x, axis=axis, keepdims=True)
    return (x - m) / jnp.sqrt(v + eps)

def _scatter_add(tgt, idx, src, axis=0):
    return tgt.at[idx].add(src)

def _segment_sum(src, seg, n):
    return jax.ops.segment_sum(src, seg, n)
kernel_name = 'mk_gps_d1_gnn_r8_8e0326'

def setup_inputs(seed: int=0):
    np.random.seed(seed)
    _w = jnp.asarray

    def _rec_inputs():
        import jax
        import jax.numpy as jnp
        _gk = jax.random.key(seed)
        x = -0.0005963 + 1.001 * jax.random.normal(jax.random.fold_in(_gk, 1), (384, 1024), jnp.float32)
        _s = jax.random.randint(jax.random.fold_in(_gk, 2), (3072,), 0, 384, jnp.int32)
        _d = jax.random.randint(jax.random.fold_in(_gk, 3), (3072,), 0, 384, jnp.int32)
        _loop = jnp.arange(384, dtype=jnp.int32)
        src = jnp.concatenate([_s, _d, _loop])
        dst = jnp.concatenate([_d, _s, _loop])
        _o = jnp.argsort(dst, stable=True)
        src = src[_o]
        dst = dst[_o]
        edge_type_5 = jax.random.randint(jax.random.fold_in(_gk, 12), (6528,), 0, 5, jnp.int32)
        return (x, src, dst, edge_type_5)
    x, src, dst, edge_type_5 = _rec_inputs()

    def _L0_gnn_setup():
        import jax, jax.numpy as jnp
        import numpy as np
        N = 384
        E = 12288
        IN_F = 1024
        OUT_F = 1024
        H = 16
        D = OUT_F // H
        NUM_ETYPES = 4

        def _build_mask(edge_index, edge_type, edge_type_weights, dtype):
            src, dst = (edge_index[0], edge_index[1])
            w = jax.nn.softplus(edge_type_weights)
            mask = jnp.full((N, N), -jnp.inf, dtype=dtype)
            mask = mask.at[src, dst].set(w[edge_type - 1])
            diag = jnp.diagonal(mask)
            idx = jnp.arange(N)
            mask = mask.at[idx, idx].set(jnp.where(jnp.isneginf(diag), w[3], diag))
            return mask
        key = jax.random.key(seed)
        ks = jax.random.split(key, 20)
        p = lambda k, shape: jax.random.normal(k, shape, dtype=jnp.float32) * 0.02
        return {'x': jax.random.normal(ks[0], (N, IN_F), dtype=jnp.float32), 'edge_index': jax.random.randint(ks[1], (2, E), 0, N), 'edge_type': jax.random.randint(ks[2], (E,), 1, NUM_ETYPES + 1), 'edge_type_weights': jnp.ones((NUM_ETYPES,), jnp.float32) + 0.1 * jax.random.normal(ks[3], (NUM_ETYPES,), dtype=jnp.float32), 'wq': p(ks[4], (OUT_F, IN_F)), 'bq': p(ks[5], (OUT_F,)), 'wk': p(ks[6], (OUT_F, IN_F)), 'bk': p(ks[7], (OUT_F,)), 'wv': p(ks[8], (OUT_F, IN_F)), 'bv': p(ks[9], (OUT_F,)), 'wiq': p(ks[10], (OUT_F, OUT_F)), 'biq': p(ks[11], (OUT_F,)), 'wik': p(ks[12], (OUT_F, OUT_F)), 'bik': p(ks[13], (OUT_F,)), 'wiv': p(ks[14], (OUT_F, OUT_F)), 'biv': p(ks[15], (OUT_F,)), 'wo': p(ks[16], (OUT_F, OUT_F)), 'bo': p(ks[17], (OUT_F,))}
    _L0_gnn_all = _L0_gnn_setup()
    _L0_gnn_in = {k: v for k, v in _L0_gnn_all.items() if k in ('edge_type_weights', 'wq', 'bq', 'wk', 'bk', 'wv', 'bv', 'wiq', 'biq', 'wik', 'bik', 'wiv', 'biv', 'wo', 'bo')}
    del _L0_gnn_all

    def _L0_mix_setup():
        import jax, jax.numpy as jnp
        import numpy as np
        HEADS = 16
        DIM_HEAD = 64
        DIM = 1024
        SCALE = DIM_HEAD ** (-0.5)
        key = jax.random.key(seed)
        ks = jax.random.split(key, 6)
        b, n = (1, 384)

        def w(k, shape, fan_in):
            return jax.random.normal(k, shape, jnp.float32) * fan_in ** (-0.5)
        x = jax.random.normal(ks[0], (b, n, DIM), jnp.float32)
        Wqkv = w(ks[1], (DIM, 3 * HEADS * DIM_HEAD), DIM)
        W1 = w(ks[2], (DIM_HEAD, DIM_HEAD), DIM_HEAD)
        b1 = jnp.zeros((DIM_HEAD,), jnp.float32)
        W2 = w(ks[3], (DIM_HEAD, 1), DIM_HEAD)
        b2 = jnp.zeros((1,), jnp.float32)
        Wout = w(ks[4], (HEADS * DIM_HEAD, DIM), HEADS * DIM_HEAD)
        bout = jnp.zeros((DIM,), jnp.float32)
        return {'x': x, 'Wqkv': Wqkv, 'W1': W1, 'b1': b1, 'W2': W2, 'b2': b2, 'Wout': Wout, 'bout': bout}
    _L0_mix_all = _L0_mix_setup()
    _L0_mix_in = {k: v for k, v in _L0_mix_all.items() if k in ('Wqkv', 'W1', 'b1', 'W2', 'b2', 'Wout', 'bout')}
    del _L0_mix_all

    def _L0_ffn_setup():
        import jax, jax.numpy as jnp
        import numpy as np
        LATENT = 1024
        LEAF_W = 64
        DEPTH = 4
        N_LEAVES = 2 ** DEPTH
        N_NODES = 2 ** DEPTH - 1
        B, S = (4, 256)

        def _fff_params(key, prefix):
            ks = jax.random.split(key, 4)
            d, h, l, n = (LATENT, LEAF_W, N_LEAVES, N_NODES)
            s_in = 1.0 / np.sqrt(d).astype(np.float32)
            s_h = 1.0 / np.sqrt(h).astype(np.float32)
            return {f'{prefix}_node_w': jax.random.normal(ks[0], (n, d), jnp.float32) * s_in, f'{prefix}_node_b': jax.random.normal(ks[1], (n,), jnp.float32) * s_in, f'{prefix}_w1': jax.random.normal(ks[2], (l, d, h), jnp.float32) * s_in, f'{prefix}_b1': jnp.zeros((l, h), jnp.float32), f'{prefix}_w2': jax.random.normal(ks[3], (l, h, d), jnp.float32) * s_h, f'{prefix}_b2': jnp.zeros((l, d), jnp.float32)}

        def _fff(x, node_w, node_b, w1, b1, w2, b2):
            Bx, Sx, D = x.shape
            xf = x.reshape(-1, D)
            N = xf.shape[0]
            cur = jnp.zeros((N,), jnp.int32)
            for _ in range(DEPTH):
                pw = node_w[cur]
                score = jnp.einsum('nd,nd->n', xf, pw) + node_b[cur]
                cur = 2 * cur + 1 + (score >= 0).astype(jnp.int32)
            leaf = cur - N_NODES
            sel = jax.nn.one_hot(leaf, N_LEAVES, dtype=xf.dtype)
            hidden_all = jax.nn.relu(jnp.einsum('nd,ldh->lnh', xf, w1) + b1[:, None, :])
            hidden = hidden_all * sel.T[:, :, None]
            out = jnp.einsum('lnh,lho->no', hidden, w2) + sel @ b2
            return out.reshape(Bx, Sx, D)
        key = jax.random.key(seed)
        kx, kq, kk, kv = jax.random.split(key, 4)
        inp = {'x': jax.random.normal(kx, (B, S, LATENT), jnp.float32)}
        inp.update(_fff_params(kq, 'q'))
        inp.update(_fff_params(kk, 'k'))
        inp.update(_fff_params(kv, 'v'))
        return inp
    _L0_ffn_all = _L0_ffn_setup()
    _L0_ffn_in = {k: v for k, v in _L0_ffn_all.items() if k in ('q_node_w', 'q_node_b', 'q_w1', 'q_b1', 'q_w2', 'q_b2', 'k_node_w', 'k_node_b', 'k_w1', 'k_b1', 'k_w2', 'k_b2', 'v_node_w', 'v_node_b', 'v_w1', 'v_b1', 'v_w2', 'v_b2')}
    del _L0_ffn_all
    return {'x': x, 'src': src, 'dst': dst, 'edge_type_5': edge_type_5, 'L0_gnn_edge_type_weights': _L0_gnn_in['edge_type_weights'], 'L0_gnn_wq': _L0_gnn_in['wq'], 'L0_gnn_bq': _L0_gnn_in['bq'], 'L0_gnn_wk': _L0_gnn_in['wk'], 'L0_gnn_bk': _L0_gnn_in['bk'], 'L0_gnn_wv': _L0_gnn_in['wv'], 'L0_gnn_bv': _L0_gnn_in['bv'], 'L0_gnn_wiq': _L0_gnn_in['wiq'], 'L0_gnn_biq': _L0_gnn_in['biq'], 'L0_gnn_wik': _L0_gnn_in['wik'], 'L0_gnn_bik': _L0_gnn_in['bik'], 'L0_gnn_wiv': _L0_gnn_in['wiv'], 'L0_gnn_biv': _L0_gnn_in['biv'], 'L0_gnn_wo': _L0_gnn_in['wo'], 'L0_gnn_bo': _L0_gnn_in['bo'], 'L0_mix_Wqkv': _L0_mix_in['Wqkv'], 'L0_mix_W1': _L0_mix_in['W1'], 'L0_mix_b1': _L0_mix_in['b1'], 'L0_mix_W2': _L0_mix_in['W2'], 'L0_mix_b2': _L0_mix_in['b2'], 'L0_mix_Wout': _L0_mix_in['Wout'], 'L0_mix_bout': _L0_mix_in['bout'], 'L0_ffn_q_node_w': _L0_ffn_in['q_node_w'], 'L0_ffn_q_node_b': _L0_ffn_in['q_node_b'], 'L0_ffn_q_w1': _L0_ffn_in['q_w1'], 'L0_ffn_q_b1': _L0_ffn_in['q_b1'], 'L0_ffn_q_w2': _L0_ffn_in['q_w2'], 'L0_ffn_q_b2': _L0_ffn_in['q_b2'], 'L0_ffn_k_node_w': _L0_ffn_in['k_node_w'], 'L0_ffn_k_node_b': _L0_ffn_in['k_node_b'], 'L0_ffn_k_w1': _L0_ffn_in['k_w1'], 'L0_ffn_k_b1': _L0_ffn_in['k_b1'], 'L0_ffn_k_w2': _L0_ffn_in['k_w2'], 'L0_ffn_k_b2': _L0_ffn_in['k_b2'], 'L0_ffn_v_node_w': _L0_ffn_in['v_node_w'], 'L0_ffn_v_node_b': _L0_ffn_in['v_node_b'], 'L0_ffn_v_w1': _L0_ffn_in['v_w1'], 'L0_ffn_v_b1': _L0_ffn_in['v_b1'], 'L0_ffn_v_w2': _L0_ffn_in['v_w2'], 'L0_ffn_v_b2': _L0_ffn_in['v_b2']}

def reference(x, src, dst, edge_type_5, L0_gnn_edge_type_weights, L0_gnn_wq, L0_gnn_bq, L0_gnn_wk, L0_gnn_bk, L0_gnn_wv, L0_gnn_bv, L0_gnn_wiq, L0_gnn_biq, L0_gnn_wik, L0_gnn_bik, L0_gnn_wiv, L0_gnn_biv, L0_gnn_wo, L0_gnn_bo, L0_mix_Wqkv, L0_mix_W1, L0_mix_b1, L0_mix_W2, L0_mix_b2, L0_mix_Wout, L0_mix_bout, L0_ffn_q_node_w, L0_ffn_q_node_b, L0_ffn_q_w1, L0_ffn_q_b1, L0_ffn_q_w2, L0_ffn_q_b2, L0_ffn_k_node_w, L0_ffn_k_node_b, L0_ffn_k_w1, L0_ffn_k_b1, L0_ffn_k_w2, L0_ffn_k_b2, L0_ffn_v_node_w, L0_ffn_v_node_b, L0_ffn_v_w1, L0_ffn_v_b1, L0_ffn_v_w2, L0_ffn_v_b2):
    import jax
    import jax.numpy as jnp

    def _L0_gnn_ref(x, edge_index, edge_type, edge_type_weights, wq, bq, wk, bk, wv, bv, wiq, biq, wik, bik, wiv, biv, wo, bo):
        import jax, jax.numpy as jnp
        import numpy as np
        N = 384
        E = 12288
        IN_F = 1024
        OUT_F = 1024
        H = 16
        D = OUT_F // H
        NUM_ETYPES = 4

        def _build_mask(edge_index, edge_type, edge_type_weights, dtype):
            src, dst = (edge_index[0], edge_index[1])
            w = jax.nn.softplus(edge_type_weights)
            mask = jnp.full((N, N), -jnp.inf, dtype=dtype)
            mask = mask.at[src, dst].set(w[edge_type - 1])
            diag = jnp.diagonal(mask)
            idx = jnp.arange(N)
            mask = mask.at[idx, idx].set(jnp.where(jnp.isneginf(diag), w[3], diag))
            return mask
        q = x @ wq.T + bq
        k = x @ wk.T + bk
        v = x @ wv.T + bv
        q2 = (q @ wiq.T + biq).reshape(N, H, D).transpose(1, 0, 2)
        k2 = (k @ wik.T + bik).reshape(N, H, D).transpose(1, 0, 2)
        v2 = (v @ wiv.T + biv).reshape(N, H, D).transpose(1, 0, 2)
        mask = _build_mask(edge_index, edge_type, edge_type_weights, x.dtype)
        scale = 1.0 / np.sqrt(D).astype(np.float32)
        scores = jnp.einsum('hnd,hmd->hnm', q2, k2) * scale + mask[None]
        attn = jax.nn.softmax(scores, axis=-1)
        out = jnp.einsum('hnm,hmd->hnd', attn, v2)
        out = out.transpose(1, 0, 2).reshape(N, OUT_F)
        return out @ wo.T + bo

    def _L0_mix_ref(x, Wqkv, W1, b1, W2, b2, Wout, bout):
        import jax, jax.numpy as jnp
        import numpy as np
        HEADS = 16
        DIM_HEAD = 64
        DIM = 1024
        SCALE = DIM_HEAD ** (-0.5)
        b, n, _ = x.shape
        qkv = x @ Wqkv
        q, k, v = jnp.split(qkv, 3, axis=-1)
        to_heads = lambda t: t.reshape(b, n, HEADS, DIM_HEAD).transpose(0, 2, 1, 3)
        q, k, v = (to_heads(q), to_heads(k), to_heads(v))
        dots = jnp.einsum('bhid,bhjd->bhij', q, k) * SCALE
        spiky = jax.nn.sigmoid(jnp.maximum(k @ W1 + b1, 0.0) @ W2 + b2)[..., 0]
        spiky_weights = jax.nn.softmax(spiky, axis=-1)
        weighted_dots = dots * spiky_weights[:, :, :, None]
        weights = jax.nn.softmax(weighted_dots, axis=-1)
        out = jnp.einsum('bhij,bhjd->bhid', weights, v)
        out = out.transpose(0, 2, 1, 3).reshape(b, n, HEADS * DIM_HEAD)
        return out @ Wout + bout

    def _L0_ffn_ref(x, q_node_w, q_node_b, q_w1, q_b1, q_w2, q_b2, k_node_w, k_node_b, k_w1, k_b1, k_w2, k_b2, v_node_w, v_node_b, v_w1, v_b1, v_w2, v_b2):
        import jax, jax.numpy as jnp
        import numpy as np
        LATENT = 1024
        LEAF_W = 64
        DEPTH = 4
        N_LEAVES = 2 ** DEPTH
        N_NODES = 2 ** DEPTH - 1
        B, S = (4, 256)

        def _fff_params(key, prefix):
            ks = jax.random.split(key, 4)
            d, h, l, n = (LATENT, LEAF_W, N_LEAVES, N_NODES)
            s_in = 1.0 / np.sqrt(d).astype(np.float32)
            s_h = 1.0 / np.sqrt(h).astype(np.float32)
            return {f'{prefix}_node_w': jax.random.normal(ks[0], (n, d), jnp.float32) * s_in, f'{prefix}_node_b': jax.random.normal(ks[1], (n,), jnp.float32) * s_in, f'{prefix}_w1': jax.random.normal(ks[2], (l, d, h), jnp.float32) * s_in, f'{prefix}_b1': jnp.zeros((l, h), jnp.float32), f'{prefix}_w2': jax.random.normal(ks[3], (l, h, d), jnp.float32) * s_h, f'{prefix}_b2': jnp.zeros((l, d), jnp.float32)}

        def _fff(x, node_w, node_b, w1, b1, w2, b2):
            Bx, Sx, D = x.shape
            xf = x.reshape(-1, D)
            N = xf.shape[0]
            cur = jnp.zeros((N,), jnp.int32)
            for _ in range(DEPTH):
                pw = node_w[cur]
                score = jnp.einsum('nd,nd->n', xf, pw) + node_b[cur]
                cur = 2 * cur + 1 + (score >= 0).astype(jnp.int32)
            leaf = cur - N_NODES
            sel = jax.nn.one_hot(leaf, N_LEAVES, dtype=xf.dtype)
            hidden_all = jax.nn.relu(jnp.einsum('nd,ldh->lnh', xf, w1) + b1[:, None, :])
            hidden = hidden_all * sel.T[:, :, None]
            out = jnp.einsum('lnh,lho->no', hidden, w2) + sel @ b2
            return out.reshape(Bx, Sx, D)
        q = _fff(x, q_node_w, q_node_b, q_w1, q_b1, q_w2, q_b2)
        k = _fff(x, k_node_w, k_node_b, k_w1, k_b1, k_w2, k_b2)
        v = _fff(x, v_node_w, v_node_b, v_w1, v_b1, v_w2, v_b2)
        scale = 1.0 / np.sqrt(LATENT).astype(np.float32)
        attn = jax.nn.softmax(jnp.einsum('bqd,bkd->bqk', q, k) * scale, axis=-1)
        return jnp.einsum('bqk,bkd->bqd', attn, v)
    edge_index = jnp.stack([src, dst])
    xn = _layernorm(x, axis=-1)
    x = x + _L0_gnn_ref(xn, edge_index, edge_type_5, L0_gnn_edge_type_weights, L0_gnn_wq, L0_gnn_bq, L0_gnn_wk, L0_gnn_bk, L0_gnn_wv, L0_gnn_bv, L0_gnn_wiq, L0_gnn_biq, L0_gnn_wik, L0_gnn_bik, L0_gnn_wiv, L0_gnn_biv, L0_gnn_wo, L0_gnn_bo) + _L0_mix_ref(xn[None], L0_mix_Wqkv, L0_mix_W1, L0_mix_b1, L0_mix_W2, L0_mix_b2, L0_mix_Wout, L0_mix_bout)[0]
    x = x + _L0_ffn_ref(_layernorm(x, axis=-1)[None], L0_ffn_q_node_w, L0_ffn_q_node_b, L0_ffn_q_w1, L0_ffn_q_b1, L0_ffn_q_w2, L0_ffn_q_b2, L0_ffn_k_node_w, L0_ffn_k_node_b, L0_ffn_k_w1, L0_ffn_k_b1, L0_ffn_k_w2, L0_ffn_k_b2, L0_ffn_v_node_w, L0_ffn_v_node_b, L0_ffn_v_w1, L0_ffn_v_b1, L0_ffn_v_w2, L0_ffn_v_b2)[0]
    return x

_drawn_inputs = setup_inputs


def setup_inputs(seed=0):
    import zlib

    import numpy as np

    out = dict(_drawn_inputs(seed))
    spreads = {'L0_mix_b1': (0.0, 0.8),
     'L0_mix_bout': (0.0, 0.1),
     'L0_ffn_q_b1': (0.0, 0.8),
     'L0_ffn_q_b2': (0.0, 0.8),
     'L0_ffn_k_b1': (0.0, 0.8),
     'L0_ffn_k_b2': (0.0, 0.8),
     'L0_ffn_v_b1': (0.0, 0.58),
     'L0_ffn_v_b2': (0.0, 0.307)}
    factors = {'L0_gnn_edge_type_weights': 5.925,
     'L0_gnn_wq': 4.366,
     'L0_gnn_bq': 8.0,
     'L0_gnn_wk': 4.295,
     'L0_gnn_bk': 8.0,
     'L0_gnn_bv': 6.168,
     'L0_gnn_wiq': 4.225,
     'L0_gnn_biq': 8.0,
     'L0_gnn_wik': 4.164,
     'L0_gnn_bik': 8.0,
     'L0_gnn_biv': 3.678,
     'L0_mix_W1': 8.0,
     'L0_mix_W2': 8.0,
     'L0_ffn_q_node_w': 2.916,
     'L0_ffn_q_node_b': 8.0,
     'L0_ffn_q_w1': 3.318,
     'L0_ffn_q_w2': 2.779,
     'L0_ffn_k_node_w': 2.824,
     'L0_ffn_k_node_b': 8.0,
     'L0_ffn_k_w1': 3.333,
     'L0_ffn_k_w2': 2.818,
     'L0_ffn_v_node_b': 5.217}
    for name, (base, spread) in spreads.items():
        noise = np.random.default_rng([zlib.crc32(name.encode()), seed]).standard_normal(out[name].shape)
        drawn = base * np.exp(spread * noise) if base else spread * noise
        out[name] = jnp.asarray(drawn.astype(out[name].dtype))
    for name, factor in factors.items():
        out[name] = (out[name] * factor).astype(out[name].dtype)
    return out
```

```python
from contextlib import ExitStack

import concourse.bass as bass
from concourse import mybir

F32 = mybir.dt.float32
F32R = mybir.dt.float32r
BF16 = mybir.dt.bfloat16
I32 = mybir.dt.int32
ALU = mybir.AluOpType
ACT = mybir.ActivationFunctionType
AX_X = mybir.AxisListType.X

P = 128
N = 384
D = 1024
NT = N // P
KT = D // P
MB = 256
GROUPS = D // MB
DH = 64
HG = MB // DH
E = 6528
ET = E // P
LEAVES = 16
EPS = 1e-5
BIG = 1e30
ATT_SCALE = DH ** -0.5
FFN_SCALE = D ** -0.5

C_BQKV, C_BIQ, C_BIK, C_BIV, C_B1, C_MB1, C_MB2, C_ETW, C_NB = 0, 24, 32, 40, 48, 72, 73, 74, 78
PP = C_NB + 48

U_QKV = 0
U_GNN = U_QKV + 3 * GROUPS
U_MIX = U_GNN + 3 * GROUPS
U_OUT = U_MIX + 3 * GROUPS
U_FFN = U_OUT + 2 * GROUPS
UNITS = U_FFN + 6 * GROUPS

LN_FILLS = KT
PRE = LN_FILLS


class Index:

    def __init__(self, base, it=None, step=0):
        self.base, self.it, self.step = base, it, step

    def __add__(self, k):
        return Index(self.base + k, self.it, self.step)

    def value(self, times=1, plus=0):
        fixed = self.base * times + plus
        return fixed if self.it is None else self.it * (self.step * times) + fixed

    def slot(self, k):
        assert self.step % k == 0
        return self.base % k

    def turn(self, k):
        assert self.step % k == 0
        return Index(self.base // k, self.it, self.step // k)


class Steps:

    def __init__(self, eng, sem):
        self.eng, self.sem, self.n, self.it, self.per = eng, sem, 0, None, 0

    def begin(self, it, per):
        self.base, self.it, self.per = self.n, it, per

    def end(self, turns):
        assert self.n - self.base == self.per, (self.n - self.base, self.per)
        self.n, self.it = self.base + self.per * turns, None

    def done(self, ins):
        self.n += 1
        ins.then_inc(self.sem, 1)
        self.eng.wait_ge(self.sem, self.n if self.it is None else self.it * self.per + self.n)


def fill_of(n):
    late = n.base >= U_FFN
    return Index(2 * n.base + PRE + (LN_FILLS if late else 0), n.it, 2 * n.step)


def t_gnn(g, h, t):
    return Index(12 * g.base + 3 * h + t, g.it, 12 * g.step)


T_MIX0 = 12 * GROUPS


def t_mix(g, k):
    return Index(T_MIX0 + 14 * g.base + k, g.it, 14 * g.step)


T_FFN0 = T_MIX0 + 14 * GROUPS


def pv_gnn(g, h):
    return Index(4 * g.base + h, g.it, 4 * g.step)


PV_MIX0 = 4 * GROUPS


def pv_mix(g, k):
    return Index(PV_MIX0 + 6 * g.base + k, g.it, 6 * g.step)


PV_NODE = PV_MIX0 + 6 * GROUPS
PV_SEL = PV_NODE + 1


def s_of(kind, g, h, t):
    return Index((0 if kind == "gnn" else 12 * GROUPS) + 12 * g.base + 3 * h + t, g.it, 12 * g.step)


S_FFN0 = 24 * GROUPS
PR = 6
TTR_START = 3.0e38


def program(nc, x, wstream, ecols, pp_in, consts, w1m, w2m, bo, bout, nodes, b2, out):
    with ExitStack() as ctx:
        def sb(name, shape, dt):
            return ctx.enter_context(nc.sbuf_tensor(name, shape, dt))

        def region(name, kib, *layouts):
            made = []
            for layout in layouts:
                with ExitStack() as s:
                    made.append([s.enter_context(nc.sbuf_tensor(n, sh, dt)) for n, sh, dt in layout])
            sb(name, [P, int(kib * 256)], F32)
            return made

        def sem(name):
            return ctx.enter_context(nc.semaphore(name))

        ident = sb("ident", [P, P], F32)
        pp = sb("pp", [P, PP], F32)
        raw = sb("raw", [P, 2, KT * MB], F32)
        w_hi = [sb(f"w_hi{s}", [P, KT, MB], F32R) for s in range(2)]
        w_lo = [sb(f"w_lo{s}", [P, KT, MB], F32R) for s in range(2)]
        xT_hi = sb("xT_hi", [P, KT, N], F32R)
        xT_lo = sb("xT_lo", [P, KT, N], F32R)
        act3 = [P, KT, N]
        (qkv_hi, qkv_lo), (oT_hi, oT_lo, o_mix, bo_b, bout_b, node_raw, node_hi, node_lo), \
            (qf_hi, qf_lo, kf_hi, kf_lo, vf_hi, vf_lo) = region(
                "region_qkv", 72.5,
                [("qkv_hi", [P, 3 * KT, N], F32R), ("qkv_lo", [P, 3 * KT, N], F32R)],
                [("oT_hi", [P, 2 * KT, N], F32R), ("oT_lo", [P, 2 * KT, N], F32R), ("o_mix", act3, F32),
                 ("bo_b", [P, D], F32), ("bout_b", [P, D], F32), ("node_raw", [P, KT, 48], F32),
                 ("node_hi", [P, KT, 48], F32R), ("node_lo", [P, KT, 48], F32R)],
                [("qf_hi", act3, F32R), ("qf_lo", act3, F32R), ("kf_hi", act3, F32R), ("kf_lo", act3, F32R),
                 ("vf_hi", [P, NT, D], F32R), ("vf_lo", [P, NT, D], F32R)])
        (onehot, iota_row, escale, ecol_i, ecol, ekey, edup, eval_, tri, junk, zeros), \
            (q_hi, q_lo, k_hi, k_lo, v_hi, v_lo), (h_lo, b2_hi0, b2_lo0, b2_hi1, b2_lo1, selT), \
            (pf_ring, pTf_hi, pTf_lo) = region(
                "region_heads", 18,
                [("onehot", [P, 2, 4, 2, N], BF16), ("iota_row", [P, N], F32), ("escale", [P, ET], F32),
                 ("ecol_i", [P, 3, ET], I32), ("ecol", [P, 3, ET], F32), ("ekey", [P, ET], F32),
                 ("edup", [P, ET], F32), ("eval", [P, ET], F32), ("tri", [P, P], F32),
                 ("junk", [P, 4, P], BF16), ("zeros", [P, N], BF16)],
                [("q_hi", [P, 2, N], F32R), ("q_lo", [P, 2, N], F32R), ("k_hi", [P, 2, N], F32R),
                 ("k_lo", [P, 2, N], F32R), ("v_hi", [P, NT, MB], F32R), ("v_lo", [P, NT, MB], F32R)],
                [("h_lo", act3, F32R), ("b2_hi0", [LEAVES, MB], F32R), ("b2_lo0", [LEAVES, MB], F32R),
                 ("b2_hi1", [LEAVES, MB], F32R), ("b2_lo1", [LEAVES, MB], F32R), ("selT", [LEAVES, N], F32R)],
                [("pf_ring", [P, NT, N], F32), ("pTf_hi", [P, NT, N], F32R), ("pTf_lo", [P, NT, N], F32R)])
        b2_hi, b2_lo = [b2_hi0, b2_hi1], [b2_lo0, b2_lo1]
        (nat,), (o_gnn,), (h_hi,), (out_sb,) = region(
            "region_nat", 12, [("nat", [P, NT, D], F32)], [("o_gnn", act3, F32)], [("h_hi", act3, F32R)],
            [("out_sb", [P, NT, D], F32)])
        (x_sb,), (p_ring, pT_hi, pT_lo), (x1, b2_raw) = region(
            "region_x", 24, [("x_sb", [P, NT, D], F32)],
            [("p_ring", [P, PR, N], F32), ("pT_hi", [P, NT, N], F32R), ("pT_lo", [P, NT, N], F32R)],
            [("x1", [P, NT, D], F32), ("b2_raw", [LEAVES, 3, D], F32)])
        (mask8,), (w1_raw, w1_hi, w1_lo, hid, w2bd, row_e), (neg_leaf, nsel, h_tmp, dec, lev1, lev2, lev3, sel) = region(
            "region_mask", 6.5, [("mask8", [P, NT, N], F32)],
            [("w1_raw", [P, P], F32), ("w1_hi", [P, P], F32R), ("w1_lo", [P, P], F32R), ("hid", [P, 2, N], F32),
             ("w2bd", [P, 2, HG], F32), ("row_e", [HG, N], F32)],
            [("neg_leaf", [P, D], BF16), ("nsel", [P, N], BF16), ("h_tmp", [P, N], F32),
             ("dec", [P, NT, 3, LEAVES], F32), ("lev1", [P, NT * 3, 2], F32), ("lev2", [P, NT * 3, 4], F32),
             ("lev3", [P, NT * 3, 8], F32), ("sel", [P, NT * 3, LEAVES], F32)])
        small = sb("small", [P, 160], F32)
        nbias, esum, rsum = small[:, 0:PR], small[:, PR:2 * PR], small[:, 2 * PR:3 * PR]
        alpha, nalpha = small[:, 18:30], small[:, 30:42]
        rowneg, rowsum, rowinv = (small[:, c:c + 1] for c in range(42, 45))
        w8, wtmp, wtmp2 = small[:, 48:52], small[:, 52:56], small[:, 56:60]
        mv = small[:, 60:66].rearrange("p (t c) -> p t c", c=2)
        ve, rec, rstd, ntmp = (small[:, 66 + 3 * i:69 + 3 * i] for i in range(4))
        stats = small[:, 80:116].rearrange("p (t c) -> p t c", t=NT)
        etmp = sb("etmp", [P, ET], F32)

        def bank(name):
            return ctx.enter_context(nc.psum_tensor(name, [P, 512], F32))

        g_bank = [bank(f"g_bank{i}") for i in range(2)]
        s_bank = [bank(f"s_bank{i}") for i in range(3)]
        t_bank = [bank(f"t_bank{i}") for i in range(2)]
        o_bank = bank("o_bank")

        x_in, small_in, late_in = sem("x_in"), sem("small_in"), sem("late_in")
        w1_in, x1_in, bias_in = sem("w1_in"), sem("x1_in"), sem("bias_in")
        raw_in = [sem("raw_in0"), sem("raw_in1")]
        consts_ready = sem("consts_ready")
        w_hi_ready, w_lo_ready = sem("w_hi_ready"), sem("w_lo_ready")
        g_full = sem("g_full")
        g_hi = sem("g_hi")
        g_free = sem("g_free")
        s_full = sem("s_full")
        e_in = sem("e_in")
        e_done = sem("e_done")
        p_ready = sem("p_ready")
        t_full, t_hi = sem("t_full"), sem("t_hi")
        t_free = sem("t_free")
        o_full = sem("o_full")
        o_free = sem("o_free")
        key_ready, key_full, key_free = sem("key_ready"), sem("key_full"), sem("key_free")
        edges_ready = sem("edges_ready")
        oh_ready, oh_free = sem("oh_ready"), sem("oh_free")
        mask_full, mask_ready = sem("mask_full"), sem("mask_ready")
        soft_a, soft_v = sem("soft_a"), sem("soft_v")
        ln_v, ln_a = sem("ln_v"), sem("ln_a")
        hid_ready = sem("hid_ready")
        row_v, row_a_sem = sem("row_v"), sem("row_a_sem")
        w1_ready = sem("w1_ready")
        split_done = sem("split_done")
        node_ready, node_hi_ready, sel_ready = sem("node_ready"), sem("node_hi_ready"), sem("sel_ready")
        sel_taken = sem("sel_taken")
        leaf_ready = sem("leaf_ready")
        selT_ready = sem("selT_ready")
        b2_hi_ready, b2_ready = sem("b2_hi_ready"), sem("b2_ready")
        out_ready, out_done = sem("out_ready"), sem("out_done")
        dve_step, act_step, pool_step = sem("dve_step"), sem("act_step"), sem("pool_step")

        block = ctx.enter_context(nc.Block())

        def flat(a):
            return a.rearrange("p a b -> p (a b)")

        @block.sync
        def _(sp):
            for s in range(2):
                sp.dma_start(raw[:, s, :], wstream[s]).then_inc(raw_in[s], 16)
            with sp.Fori(1, UNITS // 2) as i:
                for s in range(2):
                    sp.wait_ge(w_lo_ready, i * 2 + (s - 1))
                    sp.dma_start(raw[:, s, :], wstream[bass.ds(i * 2 + s, 1), :, :].rearrange("a p m -> p (a m)")) \
                      .then_inc(raw_in[s], 16)
            for t in range(NT):
                sp.wait_ge(out_ready, 2 * (t + 1))
                sp.dma_start(out[t * P:(t + 1) * P, :], out_sb[:, t, :]).then_inc(out_done, 16)
            sp.wait_ge(out_done, 16 * NT)

        @block.gpsimd
        def _(pool):
            own = Steps(pool, pool_step)
            nc.gpsimd.memset(zeros[:, :], 0.0)
            own.done(nc.gpsimd.memset(ident[:, :], 0.0))
            nc.gpsimd.affine_select(out=ident[:, :], in_=ident[:, :], compare_op=ALU.not_equal, fill=1.0, base=0,
                                    pattern=[[-1, P]], channel_multiplier=1).then_inc(consts_ready, 1)
            own.done(nc.gpsimd.memset(tri[:, :], 1.0))
            nc.gpsimd.affine_select(out=tri[:, :], in_=tri[:, :], compare_op=ALU.is_gt, fill=0.0, base=0,
                                    pattern=[[1, P]], channel_multiplier=-1).then_inc(consts_ready, 1)

            eye = p_ring[:, 3:6, :]
            pool.wait_ge(ln_v, 2)
            own.done(nc.gpsimd.memset(eye, 0.0))
            for t in range(NT):
                ins = nc.gpsimd.affine_select(out=p_ring[:, 3 + t, :], in_=p_ring[:, 3 + t, :],
                                              compare_op=ALU.not_equal, fill=1.0, base=t * P,
                                              pattern=[[-1, N]], channel_multiplier=1)
            own.done(ins)
            own.done(nc.gpsimd.tensor_scalar(mask8[:, :, :], eye, -1.0, BIG, ALU.add, ALU.mult))
            pool.wait_ge(soft_v, 3)
            own.done(nc.gpsimd.tensor_scalar(eye, eye, w8[:, 3:4], None, ALU.mult))
            nc.gpsimd.tensor_tensor(mask8[:, :, :], mask8[:, :, :], eye, ALU.add).then_inc(mask_ready, 1)

            pool.wait_ge(e_done, 3 + 12 * GROUPS)
            nc.gpsimd.memset(w1_raw[:, :], 0.0)
            own.done(nc.gpsimd.memset(w2bd[:, :, :], 0.0))
            for a in range(2):
                r = slice(a * DH, (a + 1) * DH)
                pool.dma_start(w1_raw[r, r], w1m).then_inc(w1_in, 16)
                for m in range(2):
                    pool.dma_start(w2bd[r, m, 2 * m + a:2 * m + a + 1], w2m).then_inc(w1_in, 16)
            pool.wait_ge(g_full, fill_of(Index(U_MIX)).value())
            pool.dma_start(bo_b[:, :], bo.partition_broadcast(P)).then_inc(bias_in, 16)
            pool.dma_start(bout_b[:, :], bout.partition_broadcast(P)).then_inc(bias_in, 16)
            pool.dma_start(node_raw[:, :, :], nodes).then_inc(bias_in, 16)
            pool.wait_ge(o_free, 1 + PV_MIX0)
            for k in range(KT):
                last = nc.gpsimd.tensor_scalar(o_gnn[:, k, :], o_gnn[:, k, :], pp[:, C_BIV + k:C_BIV + k + 1],
                                               None, ALU.add)
            own.done(last)
            own.done(nc.gpsimd.tensor_copy(flat(oT_hi[:, 0:KT, :]), flat(o_gnn[:, :, :])))
            nc.gpsimd.tensor_tensor(flat(oT_lo[:, 0:KT, :]), flat(o_gnn[:, :, :]), flat(oT_hi[:, 0:KT, :]),
                                    ALU.subtract).then_inc(split_done, 1)
            base = own.n
            with pool.Fori(0, GROUPS) as g:
                pool.wait_ge(o_free, g * 6 + (PV_MIX0 + 6 + 1))
                src = o_mix[:, bass.ds(g * 2, 2), :]
                nc.gpsimd.tensor_copy(oT_hi[:, bass.ds(g * 2 + KT, 2), :], src).then_inc(pool_step, 1)
                pool.wait_ge(pool_step, g * 1 + (base + 1))
                nc.gpsimd.tensor_tensor(oT_lo[:, bass.ds(g * 2 + KT, 2), :], src, oT_hi[:, bass.ds(g * 2 + KT, 2), :],
                                        ALU.subtract).then_inc(split_done, 1)
            own.n = base + GROUPS

            for t in range(NT):
                pool.dma_start(x1[:, t, :], x[t * P:(t + 1) * P, :]).then_inc(x1_in, 16)
            pool.dma_start(b2_raw[:, :, :], b2).then_inc(x1_in, 16)

            pool.wait_ge(e_done, 3 + S_FFN0)
            own.done(nc.gpsimd.memset(neg_leaf[:, :], -BIG))
            own.done(nc.gpsimd.affine_select(out=neg_leaf[:, :], in_=neg_leaf[:, :], compare_op=ALU.is_ge, fill=0.0,
                                             base=0, pattern=[[1, D]], channel_multiplier=-DH))
            nc.gpsimd.affine_select(out=neg_leaf[:, :], in_=neg_leaf[:, :], compare_op=ALU.is_ge, fill=0.0,
                                    base=DH - 1, pattern=[[-1, D]], channel_multiplier=DH).then_inc(leaf_ready, 1)
            nc.gpsimd.memset(nsel[:, :], 0.0).then_inc(leaf_ready, 1)

        @block.scalar
        def _(act):
            own = Steps(act, act_step)
            act.dma_start(pp[:, :], pp_in).then_inc(small_in, 16)
            act.dma_start(ecol_i[:, :, :], ecols).then_inc(small_in, 16)
            act.dma_start(iota_row[:, :], consts[:, 0:N]).then_inc(small_in, 16)
            act.dma_start(escale[:, :], consts[:, N:N + ET]).then_inc(small_in, 16)
            for t in range(NT):
                act.dma_start(x_sb[:, t, :], x[t * P:(t + 1) * P, :]).then_inc(x_in, 16)

            def split_hi(n):
                s = n.slot(2)
                act.wait_ge(raw_in[s], n.turn(2).value(16, 16))
                if not (n.it is None and n.base < 2):
                    act.wait_ge(g_full, fill_of(n + -1).value())
                nc.scalar.activation(flat(w_hi[s][:, :, :]), raw[:, s, :], ACT.Copy).then_inc(w_hi_ready, 1)

            def take_T(n, hi, tile, bias, func=ACT.Identity, tiles=(0, 1)):
                for m in tiles:
                    f = fill_of(n) + m
                    act.wait_ge(g_full, f.value(1, 1))
                    src = g_bank[m][:, 0:N]
                    dst = hi[:, bass.ds(tile.value(1, m), 1), :].rearrange("p a n -> p (a n)")
                    if bias is None:
                        ins = nc.scalar.activation(dst, src, ACT.Copy)
                    else:
                        ins = nc.scalar.activation(dst, src, func, bias=pp[:, bass.ds((bias + m).value(), 1)])
                    ins.then_inc(g_hi, 1)

            def take_N(n, half, hi, cols):
                act.wait_ge(g_full, (fill_of(n) + half).value(1, 1))
                t0, nt = (0, 2) if half == 0 else (2, 1)
                nc.scalar.activation(hi[:, t0:t0 + nt, cols],
                                     g_bank[half][:, 0:nt * MB].rearrange("p (t m) -> p t m", m=MB),
                                     ACT.Copy).then_inc(g_hi, 1)

            def take_norm(fill0):
                for k in range(KT):
                    act.wait_ge(g_full, fill0 + k + 1)
                    nc.scalar.activation(xT_hi[:, k, :], g_bank[k % 2][:, 0:N], ACT.Copy).then_inc(g_hi, 1)

            def root(n):
                act.wait_ge(ln_v, 2 * n + 1)
                nc.scalar.activation(rstd, rec, ACT.Sqrt).then_inc(ln_a, 1)

            def exps(kind, g, h):
                for t in range(NT):
                    q = s_of(kind, g, h, t)
                    s = q.slot(PR)
                    act.wait_ge(e_in, q.value(1, 1))
                    tile = p_ring[:, s, :]
                    if kind == "gnn":
                        ins = nc.scalar.activation(tile, tile, ACT.Exp, bias=nbias[:, s:s + 1], scale=-1.0,
                                                   accum_out=esum[:, s:s + 1])
                    else:
                        c = HG * t + h
                        ins = nc.scalar.activation(tile, s_bank[q.slot(3)][:, 0:N], ACT.Exp, bias=nbias[:, s:s + 1],
                                                   scale=alpha[:, c:c + 1], accum_out=esum[:, s:s + 1])
                    ins.then_inc(e_done, 1)

            def take_pT(tile_of):
                for t in range(NT):
                    f = tile_of(t)
                    act.wait_ge(t_full, f.value(1, 1))
                    nc.scalar.activation(pT_hi[:, :, t * P:(t + 1) * P],
                                         t_bank[f.slot(2)][:, 0:N].rearrange("p (m n) -> p m n", n=P),
                                         ACT.Copy).then_inc(t_hi, 1)

            def take_o(dst, g, h, o):
                act.wait_ge(o_full, o.value(1, 1))
                r = DH * (h % 2)
                nc.scalar.activation(dst[r:r + DH, bass.ds(g.value(2, h // 2), 1), :].rearrange("p a n -> p (a n)"),
                                     o_bank[r:r + DH, 0:N], ACT.Copy).then_inc(o_free, 1)

            act.wait_ge(soft_v, 1)
            nc.scalar.activation(wtmp, wtmp, ACT.Exp, scale=-1.0).then_inc(soft_a, 1)
            act.wait_ge(soft_v, 2)
            nc.scalar.activation(wtmp, wtmp, ACT.Ln).then_inc(soft_a, 1)
            root(0)
            split_hi(Index(0))
            take_norm(0)

            with act.Fori(0, 6) as it:
                for s in range(2):
                    n = Index(U_QKV + s, it, 2)
                    split_hi(n + 1)
                    tile = Index(2 * s, it, 4)
                    take_T(n, qkv_hi, tile, tile + C_BQKV)

            with act.Fori(0, 2) as it:
                for s in range(2):
                    g = Index(s, it, 2)
                    n = Index(U_GNN + 3 * s, it, 6)
                    zero = Index(0)
                    split_hi(n + 1)
                    take_T(n, k_hi, zero, Index(C_BIK + 2 * s, it, 4))
                    split_hi(n + 2)
                    take_T(n + 1, q_hi, zero, Index(C_BIQ + 2 * s, it, 4))
                    exps("gnn", g, 0)
                    take_N(n + 2, 0, v_hi, slice(0, MB))
                    split_hi(n + 3)
                    exps("gnn", g, 1)
                    take_N(n + 2, 1, v_hi, slice(0, MB))
                    for h in range(HG):
                        take_pT(lambda t: t_gnn(g, h, t))
                        if h < 2:
                            exps("gnn", g, h + 2)
                        take_o(o_gnn, g, h, pv_gnn(g, h))

            act.wait_ge(w1_in, 96)
            nc.scalar.activation(w1_hi[:, :], w1_raw[:, :], ACT.Copy).then_inc(w1_ready, 1)

            with act.Fori(0, 2) as it:
                for s in range(2):
                    g = Index(s, it, 2)
                    n = Index(U_MIX + 3 * s, it, 6)
                    zero = Index(0)
                    split_hi(n + 1)
                    take_T(n, k_hi, zero, None)
                    split_hi(n + 2)
                    for m in range(2):
                        take_T(n + 1, q_hi, zero, None, tiles=(m,))
                        act.wait_ge(o_full, pv_mix(g, m).value(1, 1))
                        nc.scalar.activation(hid[:, m, :], o_bank[:, 0:N], ACT.Relu,
                                             bias=pp[:, C_MB1:C_MB1 + 1]).then_inc(o_free, 1)
                    act.wait_ge(row_v, g.value(3, 1))
                    nc.scalar.activation(row_e[:, :], row_e[:, :], ACT.Exp, scale=-1.0).then_inc(t_hi, 1)
                    act.wait_ge(row_v, g.value(3, 2))
                    nc.scalar.activation(row_e[:, :], row_e[:, :], ACT.Exp, bias=rowneg[0:HG, :],
                                         accum_out=rowsum[0:HG, :]).then_inc(row_a_sem, 1)
                    take_N(n + 2, 0, v_hi, slice(0, MB))
                    act.wait_ge(t_full, t_mix(g, 1).value(1, 1))
                    nc.scalar.activation(alpha, t_bank[1][:, 0:NT * HG], ACT.Copy).then_inc(t_hi, 1)
                    act.wait_ge(t_hi, t_mix(g, 1).value(1, 1))
                    split_hi(n + 3)
                    exps("mix", g, 0)
                    take_N(n + 2, 1, v_hi, slice(0, MB))
                    exps("mix", g, 1)
                    for h in range(HG):
                        take_pT(lambda t: t_mix(g, 2 + 3 * h + t))
                        if h < 2:
                            exps("mix", g, h + 2)
                        take_o(o_mix, g, h, pv_mix(g, 2 + h))

            with act.Fori(0, GROUPS) as it:
                for s in range(2):
                    split_hi(Index(U_OUT + s + 1, it, 2))

            root(1)
            act.wait_ge(bias_in, 48)
            nc.scalar.activation(flat(node_hi[:, :, :]), flat(node_raw[:, :, :]), ACT.Copy).then_inc(node_hi_ready, 1)
            take_norm(fill_of(Index(U_FFN)).value() - LN_FILLS)

            def first_linear(f, n, tile):
                split_hi(n + 1)
                take_T(n, h_hi, tile, tile + (C_B1 + KT * f), func=ACT.Relu)

            def second_bias(f, n, cols):
                s = n.slot(2)
                nc.scalar.activation(b2_hi[s][:, :], b2_raw[:, f, cols], ACT.Copy).then_inc(b2_hi_ready, 1)

            act.wait_ge(x1_in, 64)
            for f in range(3):
                act.wait_ge(o_full, PV_SEL + f + 1)
                nc.scalar.activation(selT[:, :], o_bank[0:LEAVES, 0:N], ACT.Copy).then_inc(selT_ready, 1)
                with act.Fori(0, 2) as it:
                    for s in range(2):
                        first_linear(f, Index(U_FFN + 8 * f + s, it, 2), Index(2 * s, it, 4))
                if f < 2:
                    with act.Fori(0, 2) as it:
                        for s in range(2):
                            n = Index(U_FFN + 8 * f + 4 + s, it, 2)
                            second_bias(f, n, bass.ds(Index(MB * s, it, 2 * MB).value(), MB))
                            split_hi(n + 1)
                            take_T(n, qf_hi if f == 0 else kf_hi, Index(2 * s, it, 4), None)
            for u in range(GROUPS):
                n = Index(UNITS - GROUPS + u)
                cols = slice(u * MB, (u + 1) * MB)
                second_bias(2, n, cols)
                if u < GROUPS - 1:
                    split_hi(n + 1)
                for half in range(2):
                    take_N(n, half, vf_hi, cols)

            for t in range(NT):
                q = S_FFN0 + t
                act.wait_ge(e_in, q + 1)
                nc.scalar.activation(pf_ring[:, t, :], s_bank[q % 3][:, 0:N], ACT.Exp, bias=nbias[:, t:t + 1],
                                     scale=FFN_SCALE, accum_out=esum[:, t:t + 1]).then_inc(e_done, 1)
            for t in range(NT):
                act.wait_ge(t_full, T_FFN0 + t + 1)
                nc.scalar.activation(pTf_hi[:, :, t * P:(t + 1) * P],
                                     t_bank[t % 2][:, 0:N].rearrange("p (m n) -> p m n", n=P),
                                     ACT.Copy).then_inc(t_hi, 1)

        @block.vector
        def _(dve):
            own = Steps(dve, dve_step)
            V = nc.vector
            for c, (s, k) in enumerate(((g_free, 2), (e_done, 3), (t_free, 2), (o_free, 1), (oh_free, 2))):
                V.memset(small[:, 150 + c:151 + c], 0.0).then_inc(s, k)

            dve.wait_ge(small_in, 64)
            own.done(V.tensor_copy(flat(ecol[:, :, :]), flat(ecol_i[:, :, :])))
            V.scalar_tensor_tensor(ekey[:, :], ecol[:, 0, :], float(N), ecol[:, 1, :], ALU.mult, ALU.add) \
             .then_inc(key_ready, 1)
            etw = pp[:, C_ETW:C_ETW + 4]
            V.scalar_tensor_tensor(wtmp, etw, -1.0, etw, ALU.mult, ALU.max).then_inc(soft_v, 1)
            dve.wait_ge(soft_a, 1)
            V.tensor_scalar(wtmp, wtmp, 1.0, None, ALU.add).then_inc(soft_v, 1)
            own.done(V.tensor_scalar(etmp[:, :], ecol[:, 2, :], 1.0, 4.0, ALU.is_lt, ALU.mult))
            own.done(V.tensor_tensor(etmp[:, :], etmp[:, :], ecol[:, 2, :], ALU.add))
            own.done(V.tensor_scalar(etmp[:, :], etmp[:, :], -1.0, 0.0, ALU.add, ALU.max))
            own.done(V.tensor_scalar(etmp[:, :], etmp[:, :], 3.0, 0.25, ALU.min, ALU.mult))
            own.done(V.scalar_tensor_tensor(etmp[:, :], etmp[:, :], 1.0, escale[:, :], ALU.add, ALU.mult))
            dve.wait_ge(consts_ready, 2)
            for c in range((ET + 3) // 4):
                dve.wait_ge(key_full, c + 1)
                if c:
                    dve.wait_ge(key_free, c)
                for j in range(min(4, ET - 4 * c)):
                    e = 4 * c + j
                    last = V.scalar_tensor_tensor(junk[:, j, :], s_bank[c % 3][:, j * P:(j + 1) * P], ekey[:, e:e + 1],
                                                  tri[:, :], ALU.is_equal, ALU.mult, accum_out=edup[:, e:e + 1])
                last.then_inc(key_free, 1)
            dve.wait_ge(key_free, (ET + 3) // 4)
            V.scalar_tensor_tensor(eval_[:, :], edup[:, :], 0.0, etmp[:, :], ALU.is_equal, ALU.mult) \
             .then_inc(edges_ready, 1)
            dve.wait_ge(soft_a, 2)
            own.done(V.tensor_scalar(wtmp2, etw, 0.0, None, ALU.max))
            own.done(V.tensor_tensor(wtmp2, wtmp2, wtmp, ALU.add))
            V.tensor_scalar(w8, wtmp2, 1.0 / ATT_SCALE, None, ALU.mult).then_inc(soft_v, 1)

            def split_lo(n):
                s = n.slot(2)
                dve.wait_ge(w_hi_ready, n.value(1, 1))
                V.tensor_tensor(flat(w_lo[s][:, :, :]), raw[:, s, :], flat(w_hi[s][:, :, :]), ALU.subtract) \
                 .then_inc(w_lo_ready, 1)

            def g_hi_wait(f):
                late = f.base >= fill_of(Index(U_OUT)).value()
                dve.wait_ge(g_hi, (f + (-4 * GROUPS if late else 0)).value(1, 1))

            def take_T(n, hi, lo, tile, bias, tiles=(0, 1)):
                for m in tiles:
                    f = fill_of(n) + m
                    g_hi_wait(f)
                    src = g_bank[m][:, 0:N]
                    at = bass.ds(tile.value(1, m), 1)
                    h2, l2 = (a[:, at, :].rearrange("p a n -> p (a n)") for a in (hi, lo))
                    if bias is None:
                        ins = V.tensor_tensor(l2, src, h2, ALU.subtract)
                    else:
                        ins = V.scalar_tensor_tensor(l2, src, pp[:, bass.ds((bias + m).value(), 1)], h2,
                                                     ALU.add, ALU.subtract)
                    ins.then_inc(g_free, 1)

            def take_N(n, half, hi, lo, cols):
                g_hi_wait(fill_of(n) + half)
                t0, nt = (0, 2) if half == 0 else (2, 1)
                V.tensor_tensor(lo[:, t0:t0 + nt, cols], g_bank[half][:, 0:nt * MB].rearrange("p (t m) -> p t m", m=MB),
                                hi[:, t0:t0 + nt, cols], ALU.subtract).then_inc(g_free, 1)

            def norm(src, n):
                for t in range(NT):
                    for c in range(2):
                        last = V.bn_stats(stats[:, t, 6 * c:6 * c + 6], src[:, t, c * 512:(c + 1) * 512])
                own.done(last)
                for t in range(NT):
                    last = V.bn_aggr(mv[:, t, :], stats[:, t, :])
                own.done(last)
                own.done(V.tensor_scalar(ve, mv[:, :, 1], EPS, None, ALU.add))
                V.reciprocal(rec, ve).then_inc(ln_v, 1)
                dve.wait_ge(ln_a, n + 1)
                own.done(V.tensor_tensor(ntmp, rstd, rstd, ALU.mult))
                own.done(V.tensor_tensor(ntmp, ntmp, ve, ALU.mult))
                own.done(V.tensor_scalar(ntmp, ntmp, -0.5, 1.5, ALU.mult, ALU.add))
                own.done(V.tensor_tensor(rstd, rstd, ntmp, ALU.mult))
                for t in range(NT):
                    last = V.tensor_scalar(nat[:, t, :], src[:, t, :], mv[:, t, 0:1], rstd[:, t:t + 1],
                                           ALU.subtract, ALU.mult)
                last.then_inc(ln_v, 1)

            def take_norm(fill0):
                for k in range(KT):
                    g_hi_wait(Index(fill0 + k))
                    V.tensor_tensor(xT_lo[:, k, :], g_bank[k % 2][:, 0:N], xT_hi[:, k, :], ALU.subtract) \
                     .then_inc(g_free, 1)

            def normalise(ring, q, slot):
                dve.wait_ge(e_done, q.value(1, 4))
                own.done(V.reciprocal(rsum[:, slot:slot + 1], esum[:, slot:slot + 1]))
                V.tensor_scalar(ring[:, slot, :], ring[:, slot, :], rsum[:, slot:slot + 1], None, ALU.mult) \
                 .then_inc(p_ready, 1)

            def scores(kind, g, h):
                waiting = []
                for t in range(NT):
                    q = s_of(kind, g, h, t)
                    s = q.slot(PR)
                    dve.wait_ge(s_full, q.value(1, 1))
                    src = s_bank[q.slot(3)][:, 0:N]
                    if kind == "gnn":
                        V.memset(esum[:, s:s + 1], 0.0)
                        V.tensor_tensor_reduce(out=p_ring[:, s, :], in0=src, in1=mask8[:, t, :], scale=-ATT_SCALE,
                                               scalar=TTR_START, op0=ALU.add, op1=ALU.min,
                                               accum_out=nbias[:, s:s + 1]).then_inc(e_in, 1)
                    else:
                        c = HG * t + h
                        own.done(V.reduce_max(nbias[:, s:s + 1], src, AX_X))
                        V.tensor_tensor(nbias[:, s:s + 1], nbias[:, s:s + 1], nalpha[:, c:c + 1], ALU.mult) \
                         .then_inc(e_in, 1)
                    waiting.append((q, s))
                    if len(waiting) > 1:
                        normalise(p_ring, *waiting.pop(0))
                normalise(p_ring, *waiting.pop(0))

            def take_pT(tile_of):
                for t in range(NT):
                    f = tile_of(t)
                    dve.wait_ge(t_hi, f.value(1, 1))
                    cols = slice(t * P, (t + 1) * P)
                    V.tensor_tensor(pT_lo[:, :, cols], t_bank[f.slot(2)][:, 0:N].rearrange("p (m n) -> p m n", n=P),
                                    pT_hi[:, :, cols], ALU.subtract).then_inc(t_free, 1)

            for t in range(NT):
                dve.wait_ge(x_in, 16 * NT)
            norm(x_sb, 0)
            split_lo(Index(0))
            take_norm(0)

            def edge_tiles(slot, e, k):
                for j in range(k):
                    one = bass.ds((e + j).value(), 1)
                    V.tensor_scalar(onehot[:, slot, j, 0, :], iota_row[:, :], ecol[:, 0, one], None, ALU.is_equal)
                    last = V.tensor_scalar(onehot[:, slot, j, 1, :], iota_row[:, :], ecol[:, 1, one], eval_[:, one],
                                           ALU.is_equal, ALU.mult)
                last.then_inc(oh_ready, 1)

            dve.wait_ge(edges_ready, 1)
            with dve.Fori(0, 6) as it:
                for s in range(2):
                    n = Index(U_QKV + s, it, 2)
                    split_lo(n + 1)
                    dve.wait_ge(oh_free, it * 2 + (s + 1))
                    edge_tiles(s, Index(4 * s, it, 8), 4)
                    tile = Index(2 * s, it, 4)
                    take_T(n, qkv_hi, qkv_lo, tile, tile + C_BQKV)

            dve.wait_ge(oh_free, 13)
            edge_tiles(0, Index(48), ET - 48)

            split_lo(Index(U_GNN + 1))
            dve.wait_ge(mask_full, 1)
            dve.wait_ge(mask_ready, 1)
            code = p_ring[:, 3:6, :].bitcast(I32)
            acc, term = p_ring[:, 0:3, :], o_gnn[:, 0:3, :]
            for t in range(NT):
                last = V.tensor_scalar(code[:, t, :], s_bank[t][:, 0:N].bitcast(I32), 21, 3,
                                       ALU.logical_shift_right, ALU.bitwise_and)
            own.done(last)
            own.done(V.tensor_scalar(acc, code, 0.0, w8[:, 0:1], ALU.is_equal, ALU.mult))
            for k in range(1, 4):
                own.done(V.tensor_scalar(term, code, float(k), w8[:, k:k + 1], ALU.is_equal, ALU.mult))
                own.done(V.tensor_tensor(acc, acc, term, ALU.add))
            for t in range(NT):
                last = V.copy_predicated(mask8[:, t, :], s_bank[t][:, 0:N].bitcast(I32), acc[:, t, :])
            last.then_inc(mask_ready, 1)

            with dve.Fori(0, 2) as it:
                own.begin(it, 2 * 12)
                for s in range(2):
                    g = Index(s, it, 2)
                    n = Index(U_GNN + 3 * s, it, 6)
                    zero = Index(0)
                    take_T(n, k_hi, k_lo, zero, Index(C_BIK + 2 * s, it, 4))
                    split_lo(n + 2)
                    take_T(n + 1, q_hi, q_lo, zero, Index(C_BIQ + 2 * s, it, 4))
                    scores("gnn", g, 0)
                    take_N(n + 2, 0, v_hi, v_lo, slice(0, MB))
                    split_lo(n + 3)
                    scores("gnn", g, 1)
                    take_N(n + 2, 1, v_hi, v_lo, slice(0, MB))
                    for h in range(HG):
                        take_pT(lambda t: t_gnn(g, h, t))
                        if h < 2:
                            scores("gnn", g, h + 2)
                    split_lo(n + 4)
                own.end(2)

            dve.wait_ge(w1_ready, 1)
            V.tensor_tensor(w1_lo[:, :], w1_raw[:, :], w1_hi[:, :], ALU.subtract).then_inc(w1_ready, 1)

            with dve.Fori(0, 2) as it:
                own.begin(it, 2 * (24 + 2))
                for s in range(2):
                    g = Index(s, it, 2)
                    n = Index(U_MIX + 3 * s, it, 6)
                    zero = Index(0)
                    take_T(n, k_hi, k_lo, zero, None)
                    split_lo(n + 2)
                    take_T(n + 1, q_hi, q_lo, zero, None)
                    dve.wait_ge(t_full, t_mix(g, 0).value(1, 1))
                    V.tensor_scalar(row_e[:, :], t_bank[0][0:HG, 0:N], pp[0:HG, C_MB2:C_MB2 + 1], -80.0,
                                    ALU.add, ALU.max).then_inc(row_v, 1)
                    dve.wait_ge(t_hi, t_mix(g, 0).value(1, 1))
                    V.tensor_scalar(row_e[:, :], row_e[:, :], 1.0, None, ALU.add).then_inc(t_free, 1)
                    dve.wait_ge(t_free, t_mix(g, 0).value(1, 3))
                    own.done(V.reciprocal(row_e[:, :], row_e[:, :]))
                    V.reduce_max(rowneg[0:HG, :], row_e[:, :], AX_X, negate=True).then_inc(row_v, 1)
                    dve.wait_ge(row_a_sem, g.value(1, 1))
                    own.done(V.reciprocal(rowinv[0:HG, :], rowsum[0:HG, :]))
                    V.tensor_scalar(row_e[:, :], row_e[:, :], rowinv[0:HG, :], ATT_SCALE, ALU.mult, ALU.mult) \
                     .then_inc(row_v, 1)
                    take_N(n + 2, 0, v_hi, v_lo, slice(0, MB))
                    dve.wait_ge(t_hi, t_mix(g, 1).value(1, 1))
                    V.tensor_scalar(nalpha, t_bank[1][:, 0:NT * HG], -1.0, None, ALU.mult).then_inc(t_free, 1)
                    dve.wait_ge(t_free, t_mix(g, 1).value(1, 3))
                    split_lo(n + 3)
                    scores("mix", g, 0)
                    take_N(n + 2, 1, v_hi, v_lo, slice(0, MB))
                    scores("mix", g, 1)
                    for h in range(HG):
                        take_pT(lambda t: t_mix(g, 2 + 3 * h + t))
                        if h < 2:
                            scores("mix", g, h + 2)
                    split_lo(n + 4)
                own.end(2)

            dve.wait_ge(x1_in, 64)
            dve.wait_ge(bias_in, 48)
            own.done(V.tensor_tensor(bo_b[:, :], bo_b[:, :], bout_b[:, :], ALU.add))
            own.done(V.tensor_tensor(x1[:, :, :], x1[:, :, :], bo_b[:, None, :].to_broadcast([P, NT, D]), ALU.add))

            def add_N(n, cols):
                for half in range(2):
                    dve.wait_ge(g_full, (fill_of(n) + half).value(1, 1))
                    t0, nt = (0, 2) if half == 0 else (2, 1)
                    V.tensor_tensor(x1[:, t0:t0 + nt, cols], x1[:, t0:t0 + nt, cols],
                                    g_bank[half][:, 0:nt * MB].rearrange("p (t m) -> p t m", m=MB),
                                    ALU.add).then_inc(g_free, 1)

            with dve.Fori(0, 2) as it:
                for s in range(2):
                    n = Index(U_OUT + s, it, 2)
                    add_N(n, bass.ds(Index(s * MB, it, 2 * MB).value(), MB))
                    split_lo(n + 2)
            for u in range(GROUPS):
                add_N(Index(U_OUT + GROUPS + u), slice(u * MB, (u + 1) * MB))
                if u < GROUPS - 1:
                    split_lo(Index(U_OUT + GROUPS + u + 2))

            dve.wait_ge(g_free, fill_of(Index(U_FFN)).value() - LN_FILLS + 2)
            norm(x1, 1)
            dve.wait_ge(node_hi_ready, 1)
            V.tensor_tensor(flat(node_lo[:, :, :]), flat(node_raw[:, :, :]), flat(node_hi[:, :, :]), ALU.subtract) \
             .then_inc(node_ready, 1)
            take_norm(fill_of(Index(U_FFN)).value() - LN_FILLS)

            dve.wait_ge(o_full, PV_NODE + 1)
            dd = dec[:, :, :, :].rearrange("p t f c -> p t (f c)")
            for t in range(NT):
                last = V.tensor_tensor(dd[:, t, :], o_bank[:, t * 48:(t + 1) * 48], pp[:, C_NB:C_NB + 48], ALU.add)
            last.then_inc(o_free, 1)
            dve.wait_ge(o_free, 1 + PV_NODE + 1)
            d9 = dec[:, :, :, :].rearrange("p t f c -> p (t f) c")
            own.done(V.tensor_scalar(d9, d9, 0.0, None, ALU.is_ge))
            level = [lev1, lev2, lev3, sel]
            own.done(V.tensor_copy(level[0][:, :, 1:2], d9[:, :, 0:1]))
            own.done(V.tensor_scalar(level[0][:, :, 0:1], d9[:, :, 0:1], -1.0, 1.0, ALU.mult, ALU.add))
            for a in range(1, 4):
                w = 2 ** a
                pair = level[a][:, :, :].rearrange("p q (i c) -> p q i c", c=2)
                own.done(V.tensor_tensor(pair[:, :, :, 1], level[a - 1][:, :, :], d9[:, :, w - 1:2 * w - 1], ALU.mult))
                last = V.tensor_tensor(pair[:, :, :, 0], level[a - 1][:, :, :], pair[:, :, :, 1], ALU.subtract)
                if a < 3:
                    own.done(last)
            last.then_inc(sel_ready, 1)

            def first_linear(f, n, tile):
                split_lo(n + 1)
                for m in range(2):
                    g_hi_wait(fill_of(n) + m)
                    dve.wait_ge(g_free, (fill_of(n) + m).value(1, 2))
                    own.done(V.tensor_scalar(h_tmp[:, :], g_bank[m][:, 0:N],
                                             pp[:, bass.ds((tile + (C_B1 + KT * f + m)).value(), 1)], 0.0,
                                             ALU.add, ALU.max))
                    at = bass.ds(tile.value(1, m), 1)
                    h2, l2 = (a[:, at, :].rearrange("p a n -> p (a n)") for a in (h_hi, h_lo))
                    V.tensor_tensor(l2, h_tmp[:, :], h2, ALU.subtract).then_inc(g_free, 1)

            def second_bias(f, n, cols, k):
                s = n.slot(2)
                dve.wait_ge(b2_hi_ready, k.value(1, 1))
                V.tensor_tensor(b2_lo[s][:, :], b2_raw[:, f, cols], b2_hi[s][:, :], ALU.subtract).then_inc(b2_ready, 1)

            dve.wait_ge(leaf_ready, 2)
            for f in range(3):
                dve.wait_ge(selT_ready, f + 1)
                V.tensor_scalar(nsel[0:LEAVES, :], o_bank[0:LEAVES, 0:N], -1.0, 1.0, ALU.mult, ALU.add) \
                 .then_inc(o_free, 1)
                with dve.Fori(0, 2) as it:
                    own.begin(it, 4)
                    for s in range(2):
                        first_linear(f, Index(U_FFN + 8 * f + s, it, 2), Index(2 * s, it, 4))
                    own.end(2)
                if f < 2:
                    with dve.Fori(0, 2) as it:
                        for s in range(2):
                            n = Index(U_FFN + 8 * f + 4 + s, it, 2)
                            second_bias(f, n, bass.ds(Index(MB * s, it, 2 * MB).value(), MB),
                                        Index(4 * f + s, it, 2))
                            split_lo(n + 1)
                            out_hi, out_lo = ((qf_hi, qf_lo), (kf_hi, kf_lo))[f]
                            take_T(n, out_hi, out_lo, Index(2 * s, it, 4), None)
            for u in range(GROUPS):
                n = Index(UNITS - GROUPS + u)
                cols = slice(u * MB, (u + 1) * MB)
                second_bias(2, n, cols, Index(8 + u))
                if u < GROUPS - 1:
                    split_lo(n + 1)
                for half in range(2):
                    take_N(n, half, vf_hi, vf_lo, cols)

            for t in range(NT):
                q = S_FFN0 + t
                dve.wait_ge(s_full, q + 1)
                own.done(V.reduce_max(nbias[:, t:t + 1], s_bank[q % 3][:, 0:N], AX_X))
                V.tensor_scalar(nbias[:, t:t + 1], nbias[:, t:t + 1], -FFN_SCALE, None, ALU.mult).then_inc(e_in, 1)
                normalise(pf_ring, Index(q), t)
            for t in range(NT):
                dve.wait_ge(t_hi, T_FFN0 + t + 1)
                cols = slice(t * P, (t + 1) * P)
                V.tensor_tensor(pTf_lo[:, :, cols], t_bank[t % 2][:, 0:N].rearrange("p (m n) -> p m n", n=P),
                                pTf_hi[:, :, cols], ALU.subtract).then_inc(t_free, 1)
            for t in range(NT):
                for half in range(2):
                    cols = slice(half * 512, (half + 1) * 512)
                    dve.wait_ge(g_full, fill_of(Index(UNITS)).value() + 2 * t + half + 1)
                    V.tensor_tensor(out_sb[:, t, cols], g_bank[half][:, :], x1[:, t, cols], ALU.add) \
                     .then_inc(out_ready, 1)

        @block.tensor
        def _(pe):
            mm = nc.tensor.matmul

            def product(out, pairs):
                todo = [(a[i], b[j]) for a, b in pairs for i, j in ((0, 0), (0, 1), (1, 0))]
                for c, (a, b) in enumerate(todo):
                    last = mm(out, a, b, start=c == 0, stop=c == len(todo) - 1)
                return last

            def unit_ready(n):
                pe.wait_ge(w_lo_ready, n.value(1, 1))

            def taken(f):
                pe.wait_ge(g_free, f.value(1, 2))

            def gemm_T(n, src_hi, src_lo, k0=0, tiles=(0, 1), before=None, after=None):
                s = n.slot(2)
                for m in tiles:
                    f = fill_of(n) + m
                    if m == 0:
                        unit_ready(n)
                    pe.wait_ge(g_free, f.value(1, 1))
                    out, c = g_bank[m][:, 0:N], slice(m * P, (m + 1) * P)
                    if before:
                        before(m, out)
                    for k in range(KT):
                        w2 = (w_hi[s][:, k, c], w_lo[s][:, k, c])
                        x2 = (src_hi[:, k0 + k, :], src_lo[:, k0 + k, :])
                        for a, b in ((0, 0), (0, 1), (1, 0)):
                            last = mm(out, w2[a], x2[b], start=not before and k == 0 and a + b == 0,
                                      stop=not after and k == KT - 1 and a == 1)
                    if after:
                        last = after(m, out)
                    last.then_inc(g_full, 1)

            def gemm_N(n, src_hi, src_lo, k0, half, after=None):
                s = n.slot(2)
                if half == 0:
                    unit_ready(n)
                pe.wait_ge(g_free, (fill_of(n) + half).value(1, 1))
                for t in ((0, 1), (2,))[half]:
                    out = g_bank[half][:, (t % 2) * MB:(t % 2) * MB + MB]
                    c = slice(t * P, (t + 1) * P)
                    for k in range(KT):
                        x2 = (src_hi[:, k0 + k, c], src_lo[:, k0 + k, c])
                        w2 = (w_hi[s][:, k, :], w_lo[s][:, k, :])
                        for a, b in ((0, 0), (0, 1), (1, 0)):
                            last = mm(out, x2[a], w2[b], start=k == 0 and a + b == 0,
                                      stop=not after and k == KT - 1 and a == 1)
                    if after:
                        last = after(t, out)
                last.then_inc(g_full, 1)

            def norm_T(n, fill0):
                pe.wait_ge(ln_v, 2 * n + 2)
                for k in range(KT):
                    pe.wait_ge(g_free, fill0 + k + 1)
                    for t in range(NT):
                        last = nc.tensor.transpose(g_bank[k % 2][:, t * P:(t + 1) * P], nat[:, t, k * P:(k + 1) * P],
                                                   ident[:, :])
                    last.then_inc(g_full, 1)

            def head_scores(kind, g, h):
                r = slice(DH * (h % 2), DH * (h % 2) + DH)
                m = h // 2
                for t in range(NT):
                    q = s_of(kind, g, h, t)
                    pe.wait_ge(e_done, q.value(1, 1))
                    c = slice(t * P, (t + 1) * P)
                    product(s_bank[q.slot(3)][:, 0:N],
                            [((q_hi[r, m, c], q_lo[r, m, c]), (k_hi[r, m, :], k_lo[r, m, :]))]).then_inc(s_full, 1)

            def head_T(kind, g, h, tile_of):
                for t in range(NT):
                    q, f = s_of(kind, g, h, t), tile_of(t)
                    pe.wait_ge(p_ready, q.value(1, 1))
                    pe.wait_ge(t_free, f.value(1, 1))
                    for m in range(NT):
                        last = nc.tensor.transpose(t_bank[f.slot(2)][:, m * P:(m + 1) * P],
                                                   p_ring[:, q.slot(PR), m * P:(m + 1) * P], ident[:, :])
                    last.then_inc(t_full, 1)

            def head_out(h, last_tile, o):
                pe.wait_ge(t_free, last_tile.value(1, 3))
                pe.wait_ge(o_free, o.value(1, 1))
                c = slice((h // 2) * P, (h // 2 + 1) * P)
                product(o_bank[:, 0:N], [((v_hi[:, m, c], v_lo[:, m, c]), (pT_hi[:, m, :], pT_lo[:, m, :]))
                                         for m in range(NT)]).then_inc(o_full, 1)

            pe.wait_ge(consts_ready, 1)
            pe.wait_ge(key_ready, 1)
            for c in range((ET + 3) // 4):
                if c >= 3:
                    pe.wait_ge(key_free, c - 2)
                for j in range(min(4, ET - 4 * c)):
                    e = 4 * c + j
                    last = nc.tensor.transpose(s_bank[c % 3][:, j * P:(j + 1) * P],
                                               ekey[:, e:e + 1].to_broadcast([P, P]), ident[:, :])
                last.then_inc(key_full, 1)

            norm_T(0, 0)

            def mask_tile(slot, j, last_one=False):
                for t in range(NT):
                    last = mm(s_bank[t][:, 0:N], onehot[:, slot, j, 0, t * P:(t + 1) * P], onehot[:, slot, j, 1, :],
                              start=False, stop=last_one, skip_group_check=True)
                return last

            pe.wait_ge(key_free, (ET + 3) // 4)
            for t in range(NT):
                mm(s_bank[t][:, 0:N], zeros[:, 0:P], zeros[:, :], start=True, stop=False, skip_group_check=True)
            taken(fill_of(Index(0)))
            with pe.Fori(0, 6) as it:
                for s in range(2):
                    gemm_T(Index(U_QKV + s, it, 2), xT_hi, xT_lo)
                    pe.wait_ge(oh_ready, it * 2 + (s + 1))
                    for j in range(4):
                        last = mask_tile(s, j)
                    last.then_inc(oh_free, 1)
            pe.wait_ge(oh_ready, 13)
            for j in range(ET - 48):
                last = mask_tile(0, j, j == ET - 49)
            last.then_inc(mask_full, 1)

            with pe.Fori(0, 2) as it:
                for s in range(2):
                    g = Index(s, it, 2)
                    n = Index(U_GNN + 3 * s, it, 6)
                    if s == 0:
                        taken(fill_of(Index(U_QKV + 2 * GROUPS)))
                    gemm_T(n, qkv_hi, qkv_lo, KT)
                    gemm_T(n + 1, qkv_hi, qkv_lo, 0)
                    taken(fill_of(n + 2))
                    pe.wait_ge(mask_ready, 2)
                    head_scores("gnn", g, 0)
                    gemm_N(n + 2, qkv_hi, qkv_lo, 2 * KT, 0)
                    head_scores("gnn", g, 1)
                    gemm_N(n + 2, qkv_hi, qkv_lo, 2 * KT, 1)
                    for h in range(HG):
                        head_T("gnn", g, h, lambda t: t_gnn(g, h, t))
                        if h < 2:
                            head_scores("gnn", g, h + 2)
                        if h == 0:
                            taken(fill_of(n + 3))
                        head_out(h, t_gnn(g, h, 2), pv_gnn(g, h))

            pe.wait_ge(w1_ready, 2)
            with pe.Fori(0, 2) as it:
                for s in range(2):
                    g = Index(s, it, 2)
                    n = Index(U_MIX + 3 * s, it, 6)
                    gemm_T(n, xT_hi, xT_lo)
                    for m in range(2):
                        gemm_T(n + 1, xT_hi, xT_lo, tiles=(m,))
                        if m == 0:
                            taken(fill_of(n + 1))
                        pe.wait_ge(o_free, pv_mix(g, m).value(1, 1))
                        product(o_bank[:, 0:N], [((w1_hi[:, :], w1_lo[:, :]), (k_hi[:, m, :], k_lo[:, m, :]))]) \
                            .then_inc(o_full, 1)
                    taken(fill_of(n + 2))
                    head_scores("mix", g, 0)
                    pe.wait_ge(o_free, pv_mix(g, 1).value(1, 2))
                    pe.wait_ge(t_free, t_mix(g, 0).value(1, 1))
                    for m in range(2):
                        last = mm(t_bank[0][0:HG, 0:N], w2bd[:, m, :], hid[:, m, :], start=m == 0, stop=m == 1)
                    last.then_inc(t_full, 1)
                    gemm_N(n + 2, xT_hi, xT_lo, 0, 0)
                    pe.wait_ge(row_v, g.value(3, 3))
                    pe.wait_ge(t_free, t_mix(g, 1).value(1, 1))
                    for t in range(NT):
                        last = mm(t_bank[1][:, t * HG:(t + 1) * HG], row_e[:, t * P:(t + 1) * P], ident[0:HG, 0:HG],
                                  start=True, stop=True)
                    last.then_inc(t_full, 1)
                    gemm_N(n + 2, xT_hi, xT_lo, 0, 1)
                    head_scores("mix", g, 1)
                    for h in range(HG):
                        head_T("mix", g, h, lambda t: t_mix(g, 2 + 3 * h + t))
                        if h < 2:
                            head_scores("mix", g, h + 2)
                        if h == 0:
                            taken(fill_of(n + 3))
                        head_out(h, t_mix(g, 4 + 3 * h), pv_mix(g, 2 + h))

            for b in range(2):
                pe.wait_ge(split_done, (1, 1 + GROUPS)[b])
                with pe.Fori(0, 2) as it:
                    for s in range(2):
                        n = Index(U_OUT + 4 * b + s, it, 2)
                        for half in range(2):
                            gemm_N(n, oT_hi, oT_lo, b * KT, half)

            norm_T(1, fill_of(Index(U_FFN)).value() - LN_FILLS)
            taken(fill_of(Index(U_FFN)))
            pe.wait_ge(node_ready, 1)
            pe.wait_ge(o_free, PV_NODE + 1)
            for t in range(NT):
                c = slice(t * P, (t + 1) * P)
                last = product(o_bank[:, t * 48:(t + 1) * 48],
                               [((xT_hi[:, k, c], xT_lo[:, k, c]), (node_hi[:, k, :], node_lo[:, k, :]))
                                for k in range(KT)])
            last.then_inc(o_full, 1)

            pe.wait_ge(sel_ready, 1)
            for f in range(3):
                pe.wait_ge(o_free, PV_SEL + f + 1)
                for t in range(NT):
                    last = nc.tensor.transpose(o_bank[0:LEAVES, t * P:(t + 1) * P], sel[:, 3 * t + f, :], ident[:, :])
                last.then_inc(o_full, 1)
                pe.wait_ge(o_free, PV_SEL + f + 2)
                with pe.Fori(0, 2) as it:
                    for s in range(2):
                        n = Index(U_FFN + 8 * f + s, it, 2)

                        def leaf_mask(m, out):
                            cols = bass.ds(Index(s * MB + m * P, it, 2 * MB).value(), P)
                            mm(out, neg_leaf[:, cols], nsel[:, :], start=True, stop=False)

                        gemm_T(n, xT_hi, xT_lo, before=leaf_mask)
                first = Index(U_FFN + 8 * f + 4)
                taken(fill_of(first))
                with pe.Fori(0, 2) as it:
                    for s in range(2):
                        n = first + s
                        n = Index(n.base, it, 2)
                        count = Index(4 * f + s, it, 2)

                        def bias_T(m, out):
                            if m == 0:
                                pe.wait_ge(b2_ready, count.value(1, 1))
                            c = slice(m * P, (m + 1) * P)
                            mm(out, b2_hi[s][:, c], selT[:, :], start=False, stop=False)
                            return mm(out, b2_lo[s][:, c], selT[:, :], start=False, stop=True)

                        def bias_N(t, out):
                            if t == 0:
                                pe.wait_ge(b2_ready, count.value(1, 1))
                            c = slice(t * P, (t + 1) * P)
                            mm(out, selT[:, c], b2_hi[s][:, :], start=False, stop=False)
                            return mm(out, selT[:, c], b2_lo[s][:, :], start=False, stop=True)

                        if f < 2:
                            gemm_T(n, h_hi, h_lo, after=bias_T)
                        else:
                            for half in range(2):
                                gemm_N(n, h_hi, h_lo, 0, half, after=bias_N)

            end = fill_of(Index(UNITS))
            for t in range(NT):
                q = S_FFN0 + t
                c = slice(t * P, (t + 1) * P)
                pe.wait_ge(e_done, q + 1)
                product(s_bank[q % 3][:, 0:N], [((qf_hi[:, k, c], qf_lo[:, k, c]), (kf_hi[:, k, :], kf_lo[:, k, :]))
                                                for k in range(KT)]).then_inc(s_full, 1)
            for t in range(NT):
                pe.wait_ge(p_ready, S_FFN0 + t + 1)
                pe.wait_ge(t_free, T_FFN0 + t + 1)
                for m in range(NT):
                    last = nc.tensor.transpose(t_bank[t % 2][:, m * P:(m + 1) * P], pf_ring[:, t, m * P:(m + 1) * P],
                                               ident[:, :])
                last.then_inc(t_full, 1)
            taken(end)
            for t in range(NT):
                c = slice(t * P, (t + 1) * P)
                pe.wait_ge(t_free, T_FFN0 + t + 3)
                for half in range(2):
                    if t:
                        pe.wait_ge(out_ready, 2 * (t - 1) + half + 1)
                    cols = slice(half * 512, (half + 1) * 512)
                    product(g_bank[half][:, :], [((pTf_hi[:, m, c], pTf_lo[:, m, c]),
                                                  (vf_hi[:, m, cols], vf_lo[:, m, cols]))
                                                 for m in range(NT)]).then_inc(g_full, 1)


def kernel(**inputs):
    import numpy as np
    import concourse.bacc as bacc
    from concourse.bass_utils import run_bass_kernel_spmd

    def arr(name):
        return np.asarray(inputs[name])

    def units(w):
        return np.ascontiguousarray(w.reshape(KT, P, GROUPS, MB).transpose(2, 1, 0, 3)).reshape(GROUPS, P, KT * MB)

    def rows(w):
        return np.ascontiguousarray(w.reshape(-1, P).T)

    def grouped(k, q, v):
        return [m[g] for g in range(GROUPS) for m in (k, q, v)]

    gnn = {k: arr("L0_gnn_" + k) for k in ("wq", "wk", "wv", "wiq", "wik", "wiv", "wo")}
    t = {k: units(w.T) for k, w in gnn.items()}
    wqkv = arr("L0_mix_Wqkv")
    mq, mk, mv_ = (units(wqkv[:, i * D:(i + 1) * D]) for i in range(3))
    first = {f: units(arr(f"L0_ffn_{f}_w1").transpose(1, 0, 2).reshape(D, D)) for f in "qkv"}
    second = {f: units(arr(f"L0_ffn_{f}_w2").reshape(D, D)) for f in "qkv"}
    stream = list(t["wq"]) + list(t["wk"]) + list(t["wv"])
    stream += grouped(t["wik"], t["wiq"], t["wiv"]) + grouped(mk, mq, mv_)
    stream += list(t["wo"]) + list(units(arr("L0_mix_Wout")))
    for f in "qkv":
        stream += list(first[f]) + list(second[f])
    wstream = np.stack(stream)
    assert wstream.shape == (UNITS, P, KT * MB)

    def wide(v):
        return np.broadcast_to(v.reshape(1, -1), (P, v.size))

    node_b = np.zeros((3, LEAVES), np.float32)
    nodes = np.zeros((3, LEAVES, D), np.float32)
    for i, f in enumerate("qkv"):
        node_b[i, :LEAVES - 1] = arr(f"L0_ffn_{f}_node_b")
        nodes[i, :LEAVES - 1] = arr(f"L0_ffn_{f}_node_w")
    pp = np.concatenate(
        [rows(arr("L0_gnn_" + b)) for b in ("bq", "bk", "bv", "biq", "bik", "biv")]
        + [rows(arr(f"L0_ffn_{f}_b1").reshape(-1)) for f in "qkv"]
        + [np.concatenate([arr("L0_mix_b1")] * 2).reshape(P, 1), wide(arr("L0_mix_b2")),
           wide(arr("L0_gnn_edge_type_weights")), wide(node_b)], axis=1)
    assert pp.shape == (P, PP)
    ecols = np.stack([arr(n).reshape(ET, P).T for n in ("src", "dst", "edge_type_5")], axis=1)
    consts = np.concatenate([wide(np.arange(N, dtype=np.float32)),
                             wide((2.0 ** (4.0 * (np.arange(ET) - 25))).astype(np.float32))], axis=1)
    arrays = {
        "x": arr("x"),
        "wstream": wstream,
        "ecols": ecols,
        "pp_in": pp,
        "consts": consts,
        "w1m": arr("L0_mix_W1"),
        "w2m": arr("L0_mix_W2"),
        "bo": arr("L0_gnn_bo"),
        "bout": arr("L0_mix_bout"),
        "nodes": nodes.reshape(3 * LEAVES, KT, P).transpose(2, 1, 0),
        "b2": np.stack([arr(f"L0_ffn_{f}_b2") for f in "qkv"], axis=1),
    }
    nc = bacc.Bacc("TRN2", target_bir_lowering=False, num_devices=1)
    args = {}
    for name, a in arrays.items():
        arrays[name] = a = np.ascontiguousarray(a)
        args[name] = nc.dram_tensor(f"{name}_dram", a.shape, mybir.dt.from_np(a.dtype), kind="ExternalInput").ap()
    args["out"] = nc.dram_tensor("out_dram", (N, D), F32, kind="ExternalOutput").ap()
    program(nc, **args)
    r = run_bass_kernel_spmd(nc, [{f"{k}_dram": a for k, a in arrays.items()}], core_ids=[0])
    return r.results[0]["out_dram"]
```

```python
from contextlib import ExitStack

import concourse.bass as bass
from concourse import mybir

F32 = mybir.dt.float32
F32R = mybir.dt.float32r
BF16 = mybir.dt.bfloat16
I32 = mybir.dt.int32
ALU = mybir.AluOpType
ACT = mybir.ActivationFunctionType
AX_X = mybir.AxisListType.X

P = 128
N = 384
D = 1024
NT = N // P
KT = D // P
MB = 256
GROUPS = D // MB
DH = 64
HG = MB // DH
E = 6528
ET = E // P
LEAVES = 16
EPS = 1e-5
BIG = 1e30
ATT_SCALE = DH ** -0.5
FFN_SCALE = D ** -0.5

C_BQKV, C_BIQ, C_BIK, C_BIV, C_B1, C_MB1, C_MB2, C_ETW, C_NB = 0, 24, 32, 40, 48, 72, 73, 74, 78
C_ZERO = C_NB + 48
PP = C_ZERO + 2

U_QKV = 0
U_GNN = U_QKV + 3 * GROUPS
U_MIX = U_GNN + 3 * GROUPS
U_OUT = U_MIX + 3 * GROUPS
U_FFN = U_OUT + 2 * GROUPS
UNITS = U_FFN + 6 * GROUPS

LN_FILLS = KT
PRE = LN_FILLS


class Index:

    def __init__(self, base, it=None, step=0):
        self.base, self.it, self.step = base, it, step

    def __add__(self, k):
        return Index(self.base + k, self.it, self.step)

    def value(self, times=1, plus=0):
        fixed = self.base * times + plus
        return fixed if self.it is None else self.it * (self.step * times) + fixed

    def slot(self, k):
        assert self.step % k == 0
        return self.base % k

    def turn(self, k):
        assert self.step % k == 0
        return Index(self.base // k, self.it, self.step // k)


class Steps:

    def __init__(self, eng, sem):
        self.eng, self.sem, self.n, self.it, self.per = eng, sem, 0, None, 0

    def begin(self, it, per):
        self.base, self.it, self.per = self.n, it, per

    def end(self, turns):
        assert self.n - self.base == self.per, (self.n - self.base, self.per)
        self.n, self.it = self.base + self.per * turns, None

    def done(self, ins):
        self.n += 1
        ins.then_inc(self.sem, 1)
        self.eng.wait_ge(self.sem, self.n if self.it is None else self.it * self.per + self.n)


def fill_of(n):
    late = n.base >= U_FFN
    return Index(2 * n.base + PRE + (LN_FILLS if late else 0), n.it, 2 * n.step)


def t_gnn(g, h, t):
    return Index(12 * g.base + 3 * h + t, g.it, 12 * g.step)


T_MIX0 = 12 * GROUPS


def t_mix(g, k):
    return Index(T_MIX0 + 14 * g.base + k, g.it, 14 * g.step)


T_FFN0 = T_MIX0 + 14 * GROUPS


def pv_gnn(g, h):
    return Index(4 * g.base + h, g.it, 4 * g.step)


PV_MIX0 = 4 * GROUPS


def pv_hid(g, m):
    return Index(PV_MIX0 + m if g.base == 0 else PV_MIX0 + 6 * g.base - 1 + m)


def pv_mix(g, h):
    return Index(PV_MIX0 + 2 + 6 * g.base + h + (2 if h == HG - 1 and g.base < GROUPS - 1 else 0))


PV_NODE = PV_MIX0 + 6 * GROUPS
PV_SEL = PV_NODE + 2


def s_of(kind, g, h, t):
    return Index((0 if kind == "gnn" else 12 * GROUPS) + 12 * g.base + 3 * h + t, g.it, 12 * g.step)


S_FFN0 = 24 * GROUPS
PR = 6
TTR_START = 3.0e38


def program(nc, x, wstream, ecols, pp_in, consts, w1m, w2m, bo, bout, nodes, b2, out):
    with ExitStack() as ctx:
        def sb(name, shape, dt):
            return ctx.enter_context(nc.sbuf_tensor(name, shape, dt))

        def region(name, kib, *layouts):
            made = []
            for layout in layouts:
                with ExitStack() as s:
                    made.append([s.enter_context(nc.sbuf_tensor(n, sh, dt)) for n, sh, dt in layout])
            sb(name, [P, int(kib * 256)], F32)
            return made

        def sem(name):
            return ctx.enter_context(nc.semaphore(name))

        ident = sb("ident", [P, P], F32)
        pp = sb("pp", [P, PP], F32)
        raw = sb("raw", [P, 2, KT * MB], F32)
        w_hi = [sb(f"w_hi{s}", [P, KT, MB], F32R) for s in range(2)]
        w_lo = [sb(f"w_lo{s}", [P, KT, MB], F32R) for s in range(2)]
        act3 = [P, KT, N]
        T_X, T_Q, T_K, T_V = 0, KT, 2 * KT, 3 * KT
        pad = [P, KT * N]
        (act_hi, act_lo), (_, oT_hi, o_mix, _, oT_lo, bo_b, bout_b, node_raw, node_hi, node_lo), \
            (_, qf_hi, kf_hi, vf_hi, _, qf_lo, kf_lo, vf_lo) = region(
                "region_act", 96.5,
                [("act_hi", [P, 4 * KT, N], F32R), ("act_lo", [P, 4 * KT, N], F32R)],
                [("x_hi_place1", pad, F32), ("oT_hi", [P, 2 * KT, N], F32R), ("o_mix", act3, F32),
                 ("x_lo_place1", pad, F32), ("oT_lo", [P, 2 * KT, N], F32R),
                 ("bo_b", [P, D], F32), ("bout_b", [P, D], F32), ("node_raw", [P, KT, 48], F32),
                 ("node_hi", [P, KT, 48], F32R), ("node_lo", [P, KT, 48], F32R)],
                [("x_hi_place2", pad, F32), ("qf_hi", act3, F32R), ("kf_hi", act3, F32R), ("vf_hi", [P, NT, D], F32R),
                 ("x_lo_place2", pad, F32), ("qf_lo", act3, F32R), ("kf_lo", act3, F32R),
                 ("vf_lo", [P, NT, D], F32R)])
        (onehot, iota_row, escale, ecol_i, ecol, ekey, edup, eval_, tri, junk, zeros), \
            (q_hi, q_lo, k_hi, k_lo, v_hi, v_lo), (h_lo, b2_hi0, b2_lo0, b2_hi1, b2_lo1, selT), \
            (pf_ring, pTf_hi, pTf_lo) = region(
                "region_heads", 18,
                [("onehot", [P, 2, 4, 2, N], BF16), ("iota_row", [P, N], F32), ("escale", [P, ET], F32),
                 ("ecol_i", [P, 3, ET], I32), ("ecol", [P, 3, ET], F32), ("ekey", [P, ET], F32),
                 ("edup", [P, ET], F32), ("eval", [P, ET], F32), ("tri", [P, P], F32),
                 ("junk", [P, 4, P], BF16), ("zeros", [P, N], BF16)],
                [("q_hi", [P, 2, N], F32R), ("q_lo", [P, 2, N], F32R), ("k_hi", [P, 2, N], F32R),
                 ("k_lo", [P, 2, N], F32R), ("v_hi", [P, NT, MB], F32R), ("v_lo", [P, NT, MB], F32R)],
                [("h_lo", act3, F32R), ("b2_hi0", [LEAVES, MB], F32R), ("b2_lo0", [LEAVES, MB], F32R),
                 ("b2_hi1", [LEAVES, MB], F32R), ("b2_lo1", [LEAVES, MB], F32R), ("selT", [LEAVES, N], F32R)],
                [("pf_ring", [P, NT, N], F32), ("pTf_hi", [P, NT, N], F32R), ("pTf_lo", [P, NT, N], F32R)])
        b2_hi, b2_lo = [b2_hi0, b2_hi1], [b2_lo0, b2_lo1]
        (nat,), (o_gnn,), (y_acc,), (h_hi,), (out_sb,) = region(
            "region_nat", 12, [("nat", [P, NT, D], F32)], [("o_gnn", act3, F32)], [("y_acc", [P, NT, D], F32)],
            [("h_hi", act3, F32R)],
            [("out_sb", [P, NT, D], F32)])
        (x_sb,), (p_ring, pT_hi, pT_lo), (x1, b2_raw) = region(
            "region_x", 24, [("x_sb", [P, NT, D], F32)],
            [("p_ring", [P, PR, N], F32), ("pT_hi", [P, NT, N], F32R), ("pT_lo", [P, NT, N], F32R)],
            [("x1", [P, NT, D], F32), ("b2_raw", [LEAVES, 3, D], F32)])
        (mask8,), (w1_raw, w1_hi, w1_lo, hid, w2bd, row_e), (neg_leaf, nsel, h_tmp, dec, lev1, lev2, lev3, sel) = region(
            "region_mask", 6.5, [("mask8", [P, NT, N], F32)],
            [("w1_raw", [P, P], F32), ("w1_hi", [P, P], F32R), ("w1_lo", [P, P], F32R), ("hid", [P, 2, N], F32),
             ("w2bd", [P, 2, HG], F32), ("row_e", [HG, N], F32)],
            [("neg_leaf", [P, D], BF16), ("nsel", [P, N], BF16), ("h_tmp", [P, N], F32),
             ("dec", [P, NT, 3, LEAVES], F32), ("lev1", [P, NT * 3, 2], F32), ("lev2", [P, NT * 3, 4], F32),
             ("lev3", [P, NT * 3, 8], F32), ("sel", [P, NT * 3, LEAVES], F32)])
        small = sb("small", [P, 160], F32)
        nbias, esum, rsum = small[:, 0:PR], small[:, PR:2 * PR], small[:, 2 * PR:3 * PR]
        alpha, nalpha = small[:, 18:30], small[:, 30:42]
        rowneg, rowsum, rowinv = (small[:, c:c + 1] for c in range(42, 45))
        w8, wtmp, wtmp2 = small[:, 48:52], small[:, 52:56], small[:, 56:60]
        mv = small[:, 60:66].rearrange("p (t c) -> p t c", c=2)
        ve, rec, rstd, ntmp = (small[:, 66 + 3 * i:69 + 3 * i] for i in range(4))
        stats = small[:, 80:152].rearrange("p (t c) -> p t c", t=NT)
        etmp = sb("etmp", [P, ET], F32)

        def bank(name):
            return ctx.enter_context(nc.psum_tensor(name, [P, 512], F32))

        g_bank = [bank(f"g_bank{i}") for i in range(2)]
        s_bank = [bank(f"s_bank{i}") for i in range(3)]
        t_bank = [bank(f"t_bank{i}") for i in range(2)]
        o_bank = bank("o_bank")

        x_in, small_in, late_in = sem("x_in"), sem("small_in"), sem("late_in")
        w1_in, x1_in, bias_in = sem("w1_in"), sem("x1_in"), sem("bias_in")
        raw_in = [sem("raw_in0"), sem("raw_in1")]
        consts_ready = sem("consts_ready")
        w_hi_ready, w_lo_ready = sem("w_hi_ready"), sem("w_lo_ready")
        g_full = sem("g_full")
        g_hi = sem("g_hi")
        g_free = sem("g_free")
        s_full = sem("s_full")
        e_in = sem("e_in")
        e_done = sem("e_done")
        p_ready = sem("p_ready")
        t_full, t_hi = sem("t_full"), sem("t_hi")
        t_free = sem("t_free")
        o_full = sem("o_full")
        o_free = sem("o_free")
        key_ready, key_full, key_free = sem("key_ready"), sem("key_full"), sem("key_free")
        edges_ready = sem("edges_ready")
        oh_ready, oh_free = sem("oh_ready"), sem("oh_free")
        mask_full, mask_ready = sem("mask_full"), sem("mask_ready")
        soft_a, soft_v = sem("soft_a"), sem("soft_v")
        ln_v, ln_a = sem("ln_v"), sem("ln_a")
        hid_ready = sem("hid_ready")
        row_v, row_a_sem = sem("row_v"), sem("row_a_sem")
        w1_ready = sem("w1_ready")
        split_done = sem("split_done")
        node_ready, node_hi_ready, sel_ready = sem("node_ready"), sem("node_hi_ready"), sem("sel_ready")
        sel_taken = sem("sel_taken")
        leaf_ready = sem("leaf_ready")
        selT_ready = sem("selT_ready")
        b2_hi_ready, b2_ready = sem("b2_hi_ready"), sem("b2_ready")
        out_ready, out_done = sem("out_ready"), sem("out_done")
        dve_step, act_step, pool_step = sem("dve_step"), sem("act_step"), sem("pool_step")

        block = ctx.enter_context(nc.Block())

        def flat(a):
            return a.rearrange("p a b -> p (a b)")

        def next_bias(col, s, it):
            return Index(col + 2, it, 4) if s == 0 else Index(col + 4, it, C_ZERO - (col + 4))

        @block.sync
        def _(sp):
            for s in range(2):
                sp.dma_start(raw[:, s, :], wstream[s]).then_inc(raw_in[s], 16)
            with sp.Fori(1, UNITS // 2) as i:
                for s in range(2):
                    sp.wait_ge(w_lo_ready, i * 2 + (s - 1))
                    sp.dma_start(raw[:, s, :], wstream[bass.ds(i * 2 + s, 1), :, :].rearrange("a p m -> p (a m)")) \
                      .then_inc(raw_in[s], 16)
            for t in range(NT):
                sp.wait_ge(out_ready, 2 * (t + 1))
                sp.dma_start(out[t * P:(t + 1) * P, :], out_sb[:, t, :]).then_inc(out_done, 16)
            sp.wait_ge(out_done, 16 * NT)

        @block.gpsimd
        def _(pool):
            own = Steps(pool, pool_step)
            nc.gpsimd.memset(zeros[:, :], 0.0)
            own.done(nc.gpsimd.memset(ident[:, :], 0.0))
            nc.gpsimd.affine_select(out=ident[:, :], in_=ident[:, :], compare_op=ALU.not_equal, fill=1.0, base=0,
                                    pattern=[[-1, P]], channel_multiplier=1).then_inc(consts_ready, 1)
            own.done(nc.gpsimd.memset(tri[:, :], 1.0))
            nc.gpsimd.affine_select(out=tri[:, :], in_=tri[:, :], compare_op=ALU.is_gt, fill=0.0, base=0,
                                    pattern=[[1, P]], channel_multiplier=-1).then_inc(consts_ready, 1)

            eye = p_ring[:, 3:6, :]
            pool.wait_ge(ln_v, 2)
            own.done(nc.gpsimd.memset(eye, 0.0))
            for t in range(NT):
                ins = nc.gpsimd.affine_select(out=p_ring[:, 3 + t, :], in_=p_ring[:, 3 + t, :],
                                              compare_op=ALU.not_equal, fill=1.0, base=t * P,
                                              pattern=[[-1, N]], channel_multiplier=1)
            own.done(ins)
            own.done(nc.gpsimd.tensor_scalar(mask8[:, :, :], eye, -1.0, BIG, ALU.add, ALU.mult))
            pool.wait_ge(soft_v, 3)
            own.done(nc.gpsimd.tensor_scalar(eye, eye, w8[:, 3:4], None, ALU.mult))
            nc.gpsimd.tensor_tensor(mask8[:, :, :], mask8[:, :, :], eye, ALU.add).then_inc(mask_ready, 1)

            pool.wait_ge(e_done, 3 + 12 * GROUPS)
            nc.gpsimd.memset(w1_raw[:, :], 0.0)
            own.done(nc.gpsimd.memset(w2bd[:, :, :], 0.0))
            for a in range(2):
                r = slice(a * DH, (a + 1) * DH)
                pool.dma_start(w1_raw[r, r], w1m).then_inc(w1_in, 16)
                for m in range(2):
                    pool.dma_start(w2bd[r, m, 2 * m + a:2 * m + a + 1], w2m).then_inc(w1_in, 16)
            pool.wait_ge(g_full, fill_of(Index(U_MIX)).value())
            pool.dma_start(bo_b[:, :], bo.partition_broadcast(P)).then_inc(bias_in, 16)
            pool.dma_start(bout_b[:, :], bout.partition_broadcast(P)).then_inc(bias_in, 16)
            pool.dma_start(node_raw[:, :, :], nodes).then_inc(bias_in, 16)
            pool.wait_ge(o_free, 1 + PV_MIX0)
            for k in range(KT):
                last = nc.gpsimd.tensor_scalar(o_gnn[:, k, :], o_gnn[:, k, :], pp[:, C_BIV + k:C_BIV + k + 1],
                                               None, ALU.add)
            own.done(last)
            own.done(nc.gpsimd.tensor_copy(flat(oT_hi[:, 0:KT, :]), flat(o_gnn[:, :, :])))
            nc.gpsimd.tensor_tensor(flat(oT_lo[:, 0:KT, :]), flat(o_gnn[:, :, :]), flat(oT_hi[:, 0:KT, :]),
                                    ALU.subtract).then_inc(split_done, 1)
            for gi in range(GROUPS):
                pool.wait_ge(o_free, pv_mix(Index(gi), HG - 1).value(1, 2))
                src = o_mix[:, 2 * gi:2 * gi + 2, :]
                dst = slice(KT + 2 * gi, KT + 2 * gi + 2)
                own.done(nc.gpsimd.tensor_copy(oT_hi[:, dst, :], src))
                nc.gpsimd.tensor_tensor(oT_lo[:, dst, :], src, oT_hi[:, dst, :], ALU.subtract) \
                  .then_inc(split_done, 1)

            for t in range(NT):
                pool.dma_start(x1[:, t, :], x[t * P:(t + 1) * P, :]).then_inc(x1_in, 16)
            pool.dma_start(b2_raw[:, :, :], b2).then_inc(x1_in, 16)

            pool.wait_ge(e_done, 3 + S_FFN0)
            own.done(nc.gpsimd.memset(neg_leaf[:, :], -BIG))
            own.done(nc.gpsimd.affine_select(out=neg_leaf[:, :], in_=neg_leaf[:, :], compare_op=ALU.is_ge, fill=0.0,
                                             base=0, pattern=[[1, D]], channel_multiplier=-DH))
            nc.gpsimd.affine_select(out=neg_leaf[:, :], in_=neg_leaf[:, :], compare_op=ALU.is_ge, fill=0.0,
                                    base=DH - 1, pattern=[[-1, D]], channel_multiplier=DH).then_inc(leaf_ready, 1)
            nc.gpsimd.memset(nsel[:, :], 0.0).then_inc(leaf_ready, 1)

        @block.scalar
        def _(act):
            own = Steps(act, act_step)
            act.dma_start(pp[:, :], pp_in).then_inc(small_in, 16)
            act.dma_start(ecol_i[:, :, :], ecols).then_inc(small_in, 16)
            act.dma_start(iota_row[:, :], consts[:, 0:N]).then_inc(small_in, 16)
            act.dma_start(escale[:, :], consts[:, N:N + ET]).then_inc(small_in, 16)
            for t in range(NT):
                act.dma_start(x_sb[:, t, :], x[t * P:(t + 1) * P, :]).then_inc(x_in, 16)

            def split_hi(n):
                s = n.slot(2)
                act.wait_ge(raw_in[s], n.turn(2).value(16, 16))
                if not (n.it is None and n.base < 2):
                    act.wait_ge(g_full, fill_of(n + -1).value())
                nc.scalar.activation(flat(w_hi[s][:, :, :]), raw[:, s, :], ACT.Copy).then_inc(w_hi_ready, 1)

            def take_T(n, hi, tile, bias, func=ACT.Identity, tiles=(0, 1)):
                for m in tiles:
                    f = fill_of(n) + m
                    act.wait_ge(g_full, f.value(1, 1))
                    src = g_bank[m][:, 0:N]
                    dst = hi[:, bass.ds(tile.value(1, m), 1), :].rearrange("p a n -> p (a n)")
                    if bias is None:
                        ins = nc.scalar.activation(dst, src, ACT.Copy)
                    else:
                        ins = nc.scalar.activation(dst, src, func, bias=pp[:, bass.ds((bias + m).value(), 1)])
                    ins.then_inc(g_hi, 1)

            def take_N(n, half, hi, cols):
                act.wait_ge(g_full, (fill_of(n) + half).value(1, 1))
                t0, nt = (0, 2) if half == 0 else (2, 1)
                nc.scalar.activation(hi[:, t0:t0 + nt, cols],
                                     g_bank[half][:, 0:nt * MB].rearrange("p (t m) -> p t m", m=MB),
                                     ACT.Copy).then_inc(g_hi, 1)

            def take_norm(fill0):
                for k in range(KT):
                    act.wait_ge(g_full, fill0 + k + 1)
                    nc.scalar.activation(act_hi[:, k, :], g_bank[k % 2][:, 0:N], ACT.Copy).then_inc(g_hi, 1)

            def root(n):
                act.wait_ge(ln_v, 2 * n + 1)
                nc.scalar.activation(rstd, rec, ACT.Sqrt).then_inc(ln_a, 1)

            def exps(kind, g, h):
                for t in range(NT):
                    q = s_of(kind, g, h, t)
                    s = q.slot(PR)
                    act.wait_ge(e_in, q.value(1, 1))
                    tile = p_ring[:, s, :]
                    if kind == "gnn":
                        ins = nc.scalar.activation(tile, tile, ACT.Exp, bias=nbias[:, s:s + 1], scale=-1.0,
                                                   accum_out=esum[:, s:s + 1])
                    else:
                        c = HG * t + h
                        ins = nc.scalar.activation(tile, s_bank[q.slot(3)][:, 0:N], ACT.Exp, bias=nbias[:, s:s + 1],
                                                   scale=alpha[:, c:c + 1], accum_out=esum[:, s:s + 1])
                    ins.then_inc(e_done, 1)

            def take_pT(tile_of, tiles=range(NT)):
                for t in tiles:
                    f = tile_of(t)
                    act.wait_ge(t_full, f.value(1, 1))
                    nc.scalar.activation(pT_hi[:, :, t * P:(t + 1) * P],
                                         t_bank[f.slot(2)][:, 0:N].rearrange("p (m n) -> p m n", n=P),
                                         ACT.Copy).then_inc(t_hi, 1)

            def take_o(dst, g, h, o):
                act.wait_ge(o_full, o.value(1, 1))
                r = DH * (h % 2)
                nc.scalar.activation(dst[r:r + DH, bass.ds(g.value(2, h // 2), 1), :].rearrange("p a n -> p (a n)"),
                                     o_bank[r:r + DH, 0:N], ACT.Copy).then_inc(o_free, 1)

            act.wait_ge(soft_v, 1)
            nc.scalar.activation(wtmp, wtmp, ACT.Exp, scale=-1.0).then_inc(soft_a, 1)
            act.wait_ge(soft_v, 2)
            nc.scalar.activation(wtmp, wtmp, ACT.Ln).then_inc(soft_a, 1)
            root(0)
            split_hi(Index(0))
            take_norm(0)

            with act.Fori(0, 6) as it:
                for s in range(2):
                    n = Index(U_QKV + s, it, 2)
                    split_hi(n + 1)
                    tile = Index(2 * s, it, 4)
                    take_T(n, act_hi, tile + T_Q, tile + C_BQKV)

            zero = Index(0)
            split_hi(Index(U_GNN + 1))
            take_T(Index(U_GNN), k_hi, zero, Index(C_BIK))
            split_hi(Index(U_GNN + 2))
            take_T(Index(U_GNN + 1), q_hi, zero, Index(C_BIQ))

            def rest_of_group(kind, g, n, t_of, o_of, dst, bias_k, bias_q, with_next=True, following=None):
                take_pT(lambda t: t_of(0, t))
                exps(kind, g, 2)
                split_hi(n + 4)
                take_o(dst, g, 0, o_of(0))
                take_pT(lambda t: t_of(1, t))
                exps(kind, g, 3)
                if with_next:
                    act.wait_ge(s_full, s_of(kind, g, 3, 2).value(1, 1))
                    take_T(n + 3, k_hi, zero, bias_k)
                take_o(dst, g, 1, o_of(1))
                take_pT(lambda t: t_of(2, t))
                split_hi(n + 5)
                if with_next:
                    take_T(n + 4, q_hi, zero, bias_q, tiles=(0,))
                take_o(dst, g, 2, o_of(2))
                take_pT(lambda t: t_of(3, t), (0, 1))
                if following:
                    following()
                take_pT(lambda t: t_of(3, t), (2,))
                if with_next:
                    take_T(n + 4, q_hi, zero, bias_q, tiles=(1,))

            with act.Fori(0, 2) as it:
                for s in range(2):
                    g = Index(s, it, 2)
                    n = Index(U_GNN + 3 * s, it, 6)
                    bias_k, bias_q = next_bias(C_BIK, s, it), next_bias(C_BIQ, s, it)
                    exps("gnn", g, 0)
                    split_hi(n + 3)
                    take_N(n + 2, 0, v_hi, slice(0, MB))
                    exps("gnn", g, 1)
                    take_N(n + 2, 1, v_hi, slice(0, MB))
                    rest_of_group("gnn", g, n, lambda h, t: t_gnn(g, h, t), lambda h: pv_gnn(g, h), o_gnn,
                                  bias_k, bias_q)
                    take_o(o_gnn, g, 3, pv_gnn(g, 3))

            act.wait_ge(w1_in, 96)
            nc.scalar.activation(w1_hi[:, :], w1_raw[:, :], ACT.Copy).then_inc(w1_ready, 1)

            def hidden(g, m):
                act.wait_ge(o_full, pv_hid(g, m).value(1, 1))
                nc.scalar.activation(hid[:, m, :], o_bank[:, 0:N], ACT.Relu,
                                     bias=pp[:, C_MB1:C_MB1 + 1]).then_inc(o_free, 1)

            def exp_row(g):
                act.wait_ge(row_v, g.value(3, 1))
                nc.scalar.activation(row_e[:, :], row_e[:, :], ACT.Exp, scale=-1.0).then_inc(t_hi, 1)

            for m in range(2):
                hidden(Index(0), m)
            exp_row(Index(0))
            for gi in range(GROUPS):
                g = Index(gi)
                n = Index(U_MIX + 3 * gi)
                more = gi < GROUPS - 1
                act.wait_ge(row_v, g.value(3, 2))
                nc.scalar.activation(row_e[:, :], row_e[:, :], ACT.Exp, bias=rowneg[0:HG, :],
                                     accum_out=rowsum[0:HG, :]).then_inc(row_a_sem, 1)
                split_hi(n + 3)
                act.wait_ge(t_full, t_mix(g, 1).value(1, 1))
                nc.scalar.activation(alpha, t_bank[1][:, 0:NT * HG], ACT.Copy).then_inc(t_hi, 1)
                act.wait_ge(t_hi, t_mix(g, 1).value(1, 1))
                exps("mix", g, 0)
                take_N(n + 2, 0, v_hi, slice(0, MB))
                exps("mix", g, 1)
                take_N(n + 2, 1, v_hi, slice(0, MB))
                rest_of_group("mix", g, n, lambda h, t: t_mix(g, 2 + 3 * h + t), lambda h: pv_mix(g, h), o_mix,
                              None, None, more, (lambda: [hidden(g + 1, m) for m in range(2)]) if more else None)
                if more:
                    exp_row(g + 1)
                take_o(o_mix, g, 3, pv_mix(g, 3))

            act.wait_ge(bias_in, 48)
            nc.scalar.activation(flat(node_hi[:, :, :]), flat(node_raw[:, :, :]), ACT.Copy).then_inc(node_hi_ready, 1)
            with act.Fori(0, 3) as it:
                for s in range(2):
                    split_hi(Index(U_OUT + s + 3, it, 2))

            root(1)
            take_norm(fill_of(Index(U_FFN)).value() - LN_FILLS)
            act.wait_ge(o_full, PV_NODE + 1)
            nc.scalar.activation(h_tmp[0:48, :], o_bank[0:48, 0:N], ACT.Copy).then_inc(o_free, 1)

            def first_linear(f, n, tile):
                split_hi(n + 1)
                take_T(n, h_hi, tile, tile + (C_B1 + KT * f), func=ACT.Relu)

            def second_bias(f, n, cols):
                s = n.slot(2)
                nc.scalar.activation(b2_hi[s][:, :], b2_raw[:, f, cols], ACT.Copy).then_inc(b2_hi_ready, 1)

            act.wait_ge(x1_in, 64)
            for f in range(3):
                act.wait_ge(o_full, PV_SEL + f + 1)
                nc.scalar.activation(selT[:, :], o_bank[0:LEAVES, 0:N], ACT.Copy).then_inc(selT_ready, 1)
                with act.Fori(0, 2) as it:
                    for s in range(2):
                        first_linear(f, Index(U_FFN + 8 * f + s, it, 2), Index(2 * s, it, 4))
                if f < 2:
                    with act.Fori(0, 2) as it:
                        for s in range(2):
                            n = Index(U_FFN + 8 * f + 4 + s, it, 2)
                            second_bias(f, n, bass.ds(Index(MB * s, it, 2 * MB).value(), MB))
                            split_hi(n + 1)
                            take_T(n, qf_hi if f == 0 else kf_hi, Index(2 * s, it, 4), None)
            for u in range(GROUPS):
                n = Index(UNITS - GROUPS + u)
                cols = slice(u * MB, (u + 1) * MB)
                second_bias(2, n, cols)
                if u < GROUPS - 1:
                    split_hi(n + 1)
                for half in range(2):
                    take_N(n, half, vf_hi, cols)

            for t in range(NT):
                q = S_FFN0 + t
                act.wait_ge(e_in, q + 1)
                nc.scalar.activation(pf_ring[:, t, :], s_bank[q % 3][:, 0:N], ACT.Exp, bias=nbias[:, t:t + 1],
                                     scale=FFN_SCALE, accum_out=esum[:, t:t + 1]).then_inc(e_done, 1)
            for t in range(NT):
                act.wait_ge(t_full, T_FFN0 + t + 1)
                nc.scalar.activation(pTf_hi[:, :, t * P:(t + 1) * P],
                                     t_bank[t % 2][:, 0:N].rearrange("p (m n) -> p m n", n=P),
                                     ACT.Copy).then_inc(t_hi, 1)

        @block.vector
        def _(dve):
            own = Steps(dve, dve_step)
            V = nc.vector
            for c, (s, k) in enumerate(((g_free, 2), (e_done, 3), (t_free, 2), (o_free, 1), (oh_free, 2))):
                V.memset(small[:, 153 + c:154 + c], 0.0).then_inc(s, k)

            dve.wait_ge(small_in, 64)
            own.done(V.tensor_copy(flat(ecol[:, :, :]), flat(ecol_i[:, :, :])))
            V.scalar_tensor_tensor(ekey[:, :], ecol[:, 0, :], float(N), ecol[:, 1, :], ALU.mult, ALU.add) \
             .then_inc(key_ready, 1)
            etw = pp[:, C_ETW:C_ETW + 4]
            V.scalar_tensor_tensor(wtmp, etw, -1.0, etw, ALU.mult, ALU.max).then_inc(soft_v, 1)
            dve.wait_ge(soft_a, 1)
            V.tensor_scalar(wtmp, wtmp, 1.0, None, ALU.add).then_inc(soft_v, 1)
            own.done(V.tensor_scalar(etmp[:, :], ecol[:, 2, :], 1.0, 4.0, ALU.is_lt, ALU.mult))
            own.done(V.tensor_tensor(etmp[:, :], etmp[:, :], ecol[:, 2, :], ALU.add))
            own.done(V.tensor_scalar(etmp[:, :], etmp[:, :], -1.0, 0.0, ALU.add, ALU.max))
            own.done(V.tensor_scalar(etmp[:, :], etmp[:, :], 3.0, 0.25, ALU.min, ALU.mult))
            own.done(V.scalar_tensor_tensor(etmp[:, :], etmp[:, :], 1.0, escale[:, :], ALU.add, ALU.mult))
            dve.wait_ge(consts_ready, 2)
            for c in range((ET + 3) // 4):
                dve.wait_ge(key_full, c + 1)
                if c:
                    dve.wait_ge(key_free, c)
                for j in range(min(4, ET - 4 * c)):
                    e = 4 * c + j
                    last = V.scalar_tensor_tensor(junk[:, j, :], s_bank[c % 3][:, j * P:(j + 1) * P], ekey[:, e:e + 1],
                                                  tri[:, :], ALU.is_equal, ALU.mult, accum_out=edup[:, e:e + 1])
                last.then_inc(key_free, 1)
            dve.wait_ge(key_free, (ET + 3) // 4)
            V.scalar_tensor_tensor(eval_[:, :], edup[:, :], 0.0, etmp[:, :], ALU.is_equal, ALU.mult) \
             .then_inc(edges_ready, 1)
            dve.wait_ge(soft_a, 2)
            own.done(V.tensor_scalar(wtmp2, etw, 0.0, None, ALU.max))
            own.done(V.tensor_tensor(wtmp2, wtmp2, wtmp, ALU.add))
            V.tensor_scalar(w8, wtmp2, 1.0 / ATT_SCALE, None, ALU.mult).then_inc(soft_v, 1)

            def split_lo(n):
                s = n.slot(2)
                dve.wait_ge(w_hi_ready, n.value(1, 1))
                V.tensor_tensor(flat(w_lo[s][:, :, :]), raw[:, s, :], flat(w_hi[s][:, :, :]), ALU.subtract) \
                 .then_inc(w_lo_ready, 1)

            def g_hi_wait(f):
                late = f.base >= fill_of(Index(U_OUT)).value()
                dve.wait_ge(g_hi, (f + (-4 * GROUPS if late else 0)).value(1, 1))

            def take_T(n, hi, lo, tile, bias, tiles=(0, 1)):
                for m in tiles:
                    f = fill_of(n) + m
                    g_hi_wait(f)
                    src = g_bank[m][:, 0:N]
                    at = bass.ds(tile.value(1, m), 1)
                    h2, l2 = (a[:, at, :].rearrange("p a n -> p (a n)") for a in (hi, lo))
                    if bias is None:
                        ins = V.tensor_tensor(l2, src, h2, ALU.subtract)
                    else:
                        ins = V.scalar_tensor_tensor(l2, src, pp[:, bass.ds((bias + m).value(), 1)], h2,
                                                     ALU.add, ALU.subtract)
                    ins.then_inc(g_free, 1)

            def take_N(n, half, hi, lo, cols):
                g_hi_wait(fill_of(n) + half)
                t0, nt = (0, 2) if half == 0 else (2, 1)
                V.tensor_tensor(lo[:, t0:t0 + nt, cols], g_bank[half][:, 0:nt * MB].rearrange("p (t m) -> p t m", m=MB),
                                hi[:, t0:t0 + nt, cols], ALU.subtract).then_inc(g_free, 1)

            def norm(src, n):
                chunks = 2 if n == 0 else GROUPS
                if n == 0:
                    for t in range(NT):
                        for c in range(2):
                            last = V.bn_stats(stats[:, t, 6 * c:6 * c + 6], src[:, t, c * 512:(c + 1) * 512])
                    own.done(last)
                for t in range(NT):
                    last = V.bn_aggr(mv[:, t, :], stats[:, t, 0:6 * chunks])
                own.done(last)
                own.done(V.tensor_scalar(ve, mv[:, :, 1], EPS, None, ALU.add))
                V.reciprocal(rec, ve).then_inc(ln_v, 1)
                dve.wait_ge(ln_a, n + 1)
                own.done(V.tensor_tensor(ntmp, rstd, rstd, ALU.mult))
                own.done(V.tensor_tensor(ntmp, ntmp, ve, ALU.mult))
                own.done(V.tensor_scalar(ntmp, ntmp, -0.5, 1.5, ALU.mult, ALU.add))
                own.done(V.tensor_tensor(rstd, rstd, ntmp, ALU.mult))
                for t in range(NT):
                    last = V.tensor_scalar(nat[:, t, :], src[:, t, :], mv[:, t, 0:1], rstd[:, t:t + 1],
                                           ALU.subtract, ALU.mult)
                last.then_inc(ln_v, 1)

            def take_norm(fill0):
                for k in range(KT):
                    g_hi_wait(Index(fill0 + k))
                    V.tensor_tensor(act_lo[:, k, :], g_bank[k % 2][:, 0:N], act_hi[:, k, :], ALU.subtract) \
                     .then_inc(g_free, 1)

            def normalise(ring, q, slot):
                dve.wait_ge(e_done, q.value(1, 4))
                own.done(V.reciprocal(rsum[:, slot:slot + 1], esum[:, slot:slot + 1]))
                V.tensor_scalar(ring[:, slot, :], ring[:, slot, :], rsum[:, slot:slot + 1], None, ALU.mult) \
                 .then_inc(p_ready, 1)

            def scores(kind, g, h):
                waiting = []
                for t in range(NT):
                    q = s_of(kind, g, h, t)
                    s = q.slot(PR)
                    dve.wait_ge(s_full, q.value(1, 1))
                    src = s_bank[q.slot(3)][:, 0:N]
                    if kind == "gnn":
                        V.memset(esum[:, s:s + 1], 0.0)
                        V.tensor_tensor_reduce(out=p_ring[:, s, :], in0=src, in1=mask8[:, t, :], scale=-ATT_SCALE,
                                               scalar=TTR_START, op0=ALU.add, op1=ALU.min,
                                               accum_out=nbias[:, s:s + 1]).then_inc(e_in, 1)
                    else:
                        c = HG * t + h
                        own.done(V.reduce_max(nbias[:, s:s + 1], src, AX_X))
                        V.tensor_tensor(nbias[:, s:s + 1], nbias[:, s:s + 1], nalpha[:, c:c + 1], ALU.mult) \
                         .then_inc(e_in, 1)
                    waiting.append((q, s))
                    if len(waiting) > 1:
                        normalise(p_ring, *waiting.pop(0))
                normalise(p_ring, *waiting.pop(0))

            def take_pT(tile_of):
                for t in range(NT):
                    f = tile_of(t)
                    dve.wait_ge(t_hi, f.value(1, 1))
                    cols = slice(t * P, (t + 1) * P)
                    V.tensor_tensor(pT_lo[:, :, cols], t_bank[f.slot(2)][:, 0:N].rearrange("p (m n) -> p m n", n=P),
                                    pT_hi[:, :, cols], ALU.subtract).then_inc(t_free, 1)

            for t in range(NT):
                dve.wait_ge(x_in, 16 * NT)
            norm(x_sb, 0)
            split_lo(Index(0))
            take_norm(0)

            def edge_tiles(slot, e, k):
                for j in range(k):
                    one = bass.ds((e + j).value(), 1)
                    V.tensor_scalar(onehot[:, slot, j, 0, :], iota_row[:, :], ecol[:, 0, one], None, ALU.is_equal)
                    last = V.tensor_scalar(onehot[:, slot, j, 1, :], iota_row[:, :], ecol[:, 1, one], eval_[:, one],
                                           ALU.is_equal, ALU.mult)
                last.then_inc(oh_ready, 1)

            dve.wait_ge(edges_ready, 1)
            with dve.Fori(0, 6) as it:
                for s in range(2):
                    n = Index(U_QKV + s, it, 2)
                    split_lo(n + 1)
                    dve.wait_ge(oh_free, it * 2 + (s + 1))
                    edge_tiles(s, Index(4 * s, it, 8), 4)
                    tile = Index(2 * s, it, 4)
                    take_T(n, act_hi, act_lo, tile + T_Q, tile + C_BQKV)

            dve.wait_ge(oh_free, 13)
            edge_tiles(0, Index(48), ET - 48)

            split_lo(Index(U_GNN + 1))
            dve.wait_ge(mask_full, 1)
            dve.wait_ge(mask_ready, 1)
            code = p_ring[:, 3:6, :].bitcast(I32)
            acc, term = p_ring[:, 0:3, :], o_gnn[:, 0:3, :]
            for t in range(NT):
                last = V.tensor_scalar(code[:, t, :], s_bank[t][:, 0:N].bitcast(I32), 21, 3,
                                       ALU.logical_shift_right, ALU.bitwise_and)
            own.done(last)
            own.done(V.tensor_scalar(acc, code, 0.0, w8[:, 0:1], ALU.is_equal, ALU.mult))
            for k in range(1, 4):
                own.done(V.tensor_scalar(term, code, float(k), w8[:, k:k + 1], ALU.is_equal, ALU.mult))
                own.done(V.tensor_tensor(acc, acc, term, ALU.add))
            for t in range(NT):
                last = V.copy_predicated(mask8[:, t, :], s_bank[t][:, 0:N].bitcast(I32), acc[:, t, :])
            last.then_inc(mask_ready, 1)

            zero = Index(0)
            take_T(Index(U_GNN), k_hi, k_lo, zero, Index(C_BIK))
            split_lo(Index(U_GNN + 2))
            take_T(Index(U_GNN + 1), q_hi, q_lo, zero, Index(C_BIQ))

            def rest_of_group(kind, g, n, t_of, bias_k, bias_q, with_next=True):
                take_pT(lambda t: t_of(0, t))
                scores(kind, g, 2)
                split_lo(n + 4)
                if not with_next:
                    keep_N(n + 3, 0)
                take_pT(lambda t: t_of(1, t))
                scores(kind, g, 3)
                if with_next:
                    take_T(n + 3, k_hi, k_lo, zero, bias_k)
                else:
                    keep_N(n + 3, 1)
                take_pT(lambda t: t_of(2, t))
                split_lo(n + 5)
                if with_next:
                    take_T(n + 4, q_hi, q_lo, zero, bias_q, tiles=(0,))
                else:
                    keep_N(n + 4, 0)
                take_pT(lambda t: t_of(3, t))
                if not with_next:
                    keep_N(n + 4, 1)

            def keep_N(n, half):
                cols = slice((n.base - U_OUT) * MB, (n.base - U_OUT + 1) * MB)
                dve.wait_ge(g_full, (fill_of(n) + half).value(1, 1))
                t0, nt = (0, 2) if half == 0 else (2, 1)
                V.tensor_copy(y_acc[:, t0:t0 + nt, cols],
                              g_bank[half][:, 0:nt * MB].rearrange("p (t m) -> p t m", m=MB)).then_inc(g_free, 1)

            with dve.Fori(0, 2) as it:
                own.begin(it, 2 * 12)
                for s in range(2):
                    g = Index(s, it, 2)
                    n = Index(U_GNN + 3 * s, it, 6)
                    bias_k, bias_q = next_bias(C_BIK, s, it), next_bias(C_BIQ, s, it)
                    scores("gnn", g, 0)
                    split_lo(n + 3)
                    take_N(n + 2, 0, v_hi, v_lo, slice(0, MB))
                    scores("gnn", g, 1)
                    take_N(n + 2, 1, v_hi, v_lo, slice(0, MB))
                    rest_of_group("gnn", g, n, lambda h, t: t_gnn(g, h, t), bias_k, bias_q)
                    take_T(n + 4, q_hi, q_lo, zero, bias_q, tiles=(1,))
                own.end(2)

            dve.wait_ge(w1_ready, 1)
            V.tensor_tensor(w1_lo[:, :], w1_raw[:, :], w1_hi[:, :], ALU.subtract).then_inc(w1_ready, 1)

            for gi in range(GROUPS):
                g = Index(gi)
                n = Index(U_MIX + 3 * gi)
                more = gi < GROUPS - 1
                dve.wait_ge(t_full, t_mix(g, 0).value(1, 1))
                V.tensor_scalar(row_e[:, :], t_bank[0][0:HG, 0:N], pp[0:HG, C_MB2:C_MB2 + 1], -80.0,
                                ALU.add, ALU.max).then_inc(row_v, 1)
                dve.wait_ge(t_hi, t_mix(g, 0).value(1, 1))
                V.tensor_scalar(row_e[:, :], row_e[:, :], 1.0, None, ALU.add).then_inc(t_free, 1)
                dve.wait_ge(t_free, t_mix(g, 0).value(1, 3))
                own.done(V.reciprocal(row_e[:, :], row_e[:, :]))
                V.reduce_max(rowneg[0:HG, :], row_e[:, :], AX_X, negate=True).then_inc(row_v, 1)
                dve.wait_ge(row_a_sem, g.value(1, 1))
                own.done(V.reciprocal(rowinv[0:HG, :], rowsum[0:HG, :]))
                V.tensor_scalar(row_e[:, :], row_e[:, :], rowinv[0:HG, :], ATT_SCALE, ALU.mult, ALU.mult) \
                 .then_inc(row_v, 1)
                split_lo(n + 3)
                dve.wait_ge(t_hi, t_mix(g, 1).value(1, 1))
                V.tensor_scalar(nalpha, t_bank[1][:, 0:NT * HG], -1.0, None, ALU.mult).then_inc(t_free, 1)
                dve.wait_ge(t_free, t_mix(g, 1).value(1, 3))
                scores("mix", g, 0)
                take_N(n + 2, 0, v_hi, v_lo, slice(0, MB))
                scores("mix", g, 1)
                take_N(n + 2, 1, v_hi, v_lo, slice(0, MB))
                rest_of_group("mix", g, n, lambda h, t: t_mix(g, 2 + 3 * h + t), None, None, more)
                if more:
                    take_T(n + 4, q_hi, q_lo, zero, None, tiles=(1,))

            dve.wait_ge(bias_in, 48)
            own.done(V.tensor_tensor(bo_b[:, :], bo_b[:, :], bout_b[:, :], ALU.add))
            for u in range(2, GROUPS):
                split_lo(Index(U_OUT + u + 1))
                for half in range(2):
                    keep_N(Index(U_OUT + u), half)
                if u == 2:
                    dve.wait_ge(x1_in, 64)
                    own.done(V.tensor_tensor(x1[:, :, :], x1[:, :, :], bo_b[:, None, :].to_broadcast([P, NT, D]),
                                             ALU.add))
            split_lo(Index(U_OUT + GROUPS + 1))
            dve.wait_ge(g_free, fill_of(Index(U_OUT + GROUPS)).value(1, 2))
            own.done(V.tensor_tensor(x1[:, :, :], x1[:, :, :], y_acc[:, :, :], ALU.add))
            dve.wait_ge(node_hi_ready, 1)
            V.tensor_tensor(flat(node_lo[:, :, :]), flat(node_raw[:, :, :]), flat(node_hi[:, :, :]), ALU.subtract) \
             .then_inc(node_ready, 1)

            def add_N(n, u, cols):
                for half in range(2):
                    dve.wait_ge(g_full, (fill_of(n) + half).value(1, 1))
                    t0, nt = (0, 2) if half == 0 else (2, 1)
                    V.tensor_tensor(x1[:, t0:t0 + nt, cols], x1[:, t0:t0 + nt, cols],
                                    g_bank[half][:, 0:nt * MB].rearrange("p (t m) -> p t m", m=MB),
                                    ALU.add).then_inc(g_free, 1)
                    dve.wait_ge(g_free, (fill_of(n) + half).value(1, 3))
                    if u == GROUPS - 1 and half == 0:
                        dve.wait_ge(ln_v, 2)
                    for t in range(t0, t0 + nt):
                        last = V.bn_stats(stats[:, t, 6 * u:6 * u + 6], x1[:, t, cols])
                return last

            for u in range(GROUPS):
                n = Index(U_OUT + GROUPS + u)
                cols = slice(u * MB, (u + 1) * MB)
                if u:
                    split_lo(n + 1)
                last = add_N(n, u, cols)
            own.done(last)
            norm(x1, 1)
            take_norm(fill_of(Index(U_FFN)).value() - LN_FILLS)

            dve.wait_ge(o_full, PV_NODE + 2)
            dd = dec[:, :, :, :].rearrange("p t f c -> p t (f c)")
            for t in range(NT):
                last = V.tensor_tensor(dd[:, t, :], o_bank[:, t * 48:(t + 1) * 48], pp[:, C_NB:C_NB + 48], ALU.add)
            last.then_inc(o_free, 1)
            dve.wait_ge(o_free, 1 + PV_NODE + 2)
            d9 = dec[:, :, :, :].rearrange("p t f c -> p (t f) c")
            own.done(V.tensor_scalar(d9, d9, 0.0, None, ALU.is_ge))
            level = [lev1, lev2, lev3, sel]
            own.done(V.tensor_copy(level[0][:, :, 1:2], d9[:, :, 0:1]))
            own.done(V.tensor_scalar(level[0][:, :, 0:1], d9[:, :, 0:1], -1.0, 1.0, ALU.mult, ALU.add))
            for a in range(1, 4):
                w = 2 ** a
                pair = level[a][:, :, :].rearrange("p q (i c) -> p q i c", c=2)
                own.done(V.tensor_tensor(pair[:, :, :, 1], level[a - 1][:, :, :], d9[:, :, w - 1:2 * w - 1], ALU.mult))
                last = V.tensor_tensor(pair[:, :, :, 0], level[a - 1][:, :, :], pair[:, :, :, 1], ALU.subtract)
                if a < 3:
                    own.done(last)
            last.then_inc(sel_ready, 1)

            def first_linear(f, n, tile):
                split_lo(n + 1)
                for m in range(2):
                    g_hi_wait(fill_of(n) + m)
                    dve.wait_ge(g_free, (fill_of(n) + m).value(1, 2))
                    own.done(V.tensor_scalar(h_tmp[:, :], g_bank[m][:, 0:N],
                                             pp[:, bass.ds((tile + (C_B1 + KT * f + m)).value(), 1)], 0.0,
                                             ALU.add, ALU.max))
                    at = bass.ds(tile.value(1, m), 1)
                    h2, l2 = (a[:, at, :].rearrange("p a n -> p (a n)") for a in (h_hi, h_lo))
                    V.tensor_tensor(l2, h_tmp[:, :], h2, ALU.subtract).then_inc(g_free, 1)

            def second_bias(f, n, cols, k):
                s = n.slot(2)
                dve.wait_ge(b2_hi_ready, k.value(1, 1))
                V.tensor_tensor(b2_lo[s][:, :], b2_raw[:, f, cols], b2_hi[s][:, :], ALU.subtract).then_inc(b2_ready, 1)

            dve.wait_ge(leaf_ready, 2)
            for f in range(3):
                dve.wait_ge(selT_ready, f + 1)
                V.tensor_scalar(nsel[0:LEAVES, :], o_bank[0:LEAVES, 0:N], -1.0, 1.0, ALU.mult, ALU.add) \
                 .then_inc(o_free, 1)
                with dve.Fori(0, 2) as it:
                    own.begin(it, 4)
                    for s in range(2):
                        first_linear(f, Index(U_FFN + 8 * f + s, it, 2), Index(2 * s, it, 4))
                    own.end(2)
                if f < 2:
                    with dve.Fori(0, 2) as it:
                        for s in range(2):
                            n = Index(U_FFN + 8 * f + 4 + s, it, 2)
                            second_bias(f, n, bass.ds(Index(MB * s, it, 2 * MB).value(), MB),
                                        Index(4 * f + s, it, 2))
                            split_lo(n + 1)
                            out_hi, out_lo = ((qf_hi, qf_lo), (kf_hi, kf_lo))[f]
                            take_T(n, out_hi, out_lo, Index(2 * s, it, 4), None)
            for u in range(GROUPS):
                n = Index(UNITS - GROUPS + u)
                cols = slice(u * MB, (u + 1) * MB)
                second_bias(2, n, cols, Index(8 + u))
                if u < GROUPS - 1:
                    split_lo(n + 1)
                for half in range(2):
                    take_N(n, half, vf_hi, vf_lo, cols)

            for t in range(NT):
                q = S_FFN0 + t
                dve.wait_ge(s_full, q + 1)
                own.done(V.reduce_max(nbias[:, t:t + 1], s_bank[q % 3][:, 0:N], AX_X))
                V.tensor_scalar(nbias[:, t:t + 1], nbias[:, t:t + 1], -FFN_SCALE, None, ALU.mult).then_inc(e_in, 1)
                normalise(pf_ring, Index(q), t)
            for t in range(NT):
                dve.wait_ge(t_hi, T_FFN0 + t + 1)
                cols = slice(t * P, (t + 1) * P)
                V.tensor_tensor(pTf_lo[:, :, cols], t_bank[t % 2][:, 0:N].rearrange("p (m n) -> p m n", n=P),
                                pTf_hi[:, :, cols], ALU.subtract).then_inc(t_free, 1)
            for t in range(NT):
                for half in range(2):
                    cols = slice(half * 512, (half + 1) * 512)
                    dve.wait_ge(g_full, fill_of(Index(UNITS)).value() + 2 * t + half + 1)
                    V.tensor_tensor(out_sb[:, t, cols], g_bank[half][:, :], x1[:, t, cols], ALU.add) \
                     .then_inc(out_ready, 1)

        @block.tensor
        def _(pe):
            mm = nc.tensor.matmul

            def product(out, pairs):
                todo = [(a[i], b[j]) for a, b in pairs for i, j in ((0, 0), (0, 1), (1, 0))]
                for c, (a, b) in enumerate(todo):
                    last = mm(out, a, b, start=c == 0, stop=c == len(todo) - 1)
                return last

            def unit_ready(n):
                pe.wait_ge(w_lo_ready, n.value(1, 1))

            def taken(f):
                pe.wait_ge(g_free, f.value(1, 2))

            def gemm_T(n, src_hi, src_lo, k0=0, tiles=(0, 1), after=None, halfway=None, at_start=None,
                       at_end=None):
                s = n.slot(2)
                for m in tiles:
                    f = fill_of(n) + m
                    if m == 0:
                        unit_ready(n)
                    pe.wait_ge(g_free, f.value(1, 1))
                    out, c = g_bank[m][:, 0:N], slice(m * P, (m + 1) * P)
                    for k in range(KT):
                        w2 = (w_hi[s][:, k, c], w_lo[s][:, k, c])
                        at = k0 + k if isinstance(k0, int) else bass.ds(k0.value(1, k), 1)
                        x2 = [a[:, at, :] if isinstance(k0, int) else a[:, at, :].rearrange("p a n -> p (a n)")
                              for a in (src_hi, src_lo)]
                        for a, b in ((0, 0), (0, 1), (1, 0)):
                            last = mm(out, w2[a], x2[b], start=k == 0 and a + b == 0,
                                      stop=not after and k == KT - 1 and a == 1)
                        if at_start and k == 1:
                            at_start()
                        if at_end and m == 0 and k == KT - 2:
                            at_end()
                        if halfway and k == (KT // 2 - 1 if not at_start else KT - 1):
                            halfway()
                    if after:
                        last = after(m, out)
                    last.then_inc(g_full, 1)

            def gemm_N(n, src_hi, src_lo, k0, half, after=None, halfway=None, at_end=None):
                s = n.slot(2)
                if half == 0:
                    unit_ready(n)
                pe.wait_ge(g_free, (fill_of(n) + half).value(1, 1))
                for t in ((0, 1), (2,))[half]:
                    out = g_bank[half][:, (t % 2) * MB:(t % 2) * MB + MB]
                    c = slice(t * P, (t + 1) * P)
                    for k in range(KT):
                        x2 = (src_hi[:, k0 + k, c], src_lo[:, k0 + k, c])
                        w2 = (w_hi[s][:, k, :], w_lo[s][:, k, :])
                        for a, b in ((0, 0), (0, 1), (1, 0)):
                            last = mm(out, x2[a], w2[b], start=k == 0 and a + b == 0,
                                      stop=not after and k == KT - 1 and a == 1)
                        if at_end and (k, t) == (KT - 2, 0):
                            at_end()
                        if halfway and (k, t) == ((KT - 1, 0), (KT // 2 - 1, 2))[half]:
                            halfway()
                    if after:
                        last = after(t, out)
                last.then_inc(g_full, 1)

            def norm_T(n, fill0, each=None):
                pe.wait_ge(ln_v, 2 * n + 2)
                for k in range(KT):
                    pe.wait_ge(g_free, fill0 + k + 1)
                    for t in range(NT):
                        last = nc.tensor.transpose(g_bank[k % 2][:, t * P:(t + 1) * P], nat[:, t, k * P:(k + 1) * P],
                                                   ident[:, :])
                    last.then_inc(g_full, 1)
                    if each and k >= 2:
                        each(k - 2)
                if each:
                    for k in (KT - 2, KT - 1):
                        pe.wait_ge(g_free, fill0 + k + 3)
                        each(k)

            def head_scores(kind, g, h):
                r = slice(DH * (h % 2), DH * (h % 2) + DH)
                m = h // 2
                for t in range(NT):
                    q = s_of(kind, g, h, t)
                    pe.wait_ge(e_done, q.value(1, 1))
                    c = slice(t * P, (t + 1) * P)
                    product(s_bank[q.slot(3)][:, 0:N],
                            [((q_hi[r, m, c], q_lo[r, m, c]), (k_hi[r, m, :], k_lo[r, m, :]))]).then_inc(s_full, 1)

            def head_T(kind, g, h, tile_of, tiles):
                for t in tiles:
                    q, f = s_of(kind, g, h, t), tile_of(t)
                    pe.wait_ge(p_ready, q.value(1, 1))
                    pe.wait_ge(t_free, f.value(1, 1))
                    for m in range(NT):
                        last = nc.tensor.transpose(t_bank[f.slot(2)][:, m * P:(m + 1) * P],
                                                   p_ring[:, q.slot(PR), m * P:(m + 1) * P], ident[:, :])
                    last.then_inc(t_full, 1)

            def head_out(h, last_tile, o):
                pe.wait_ge(t_free, last_tile.value(1, 3))
                pe.wait_ge(o_free, o.value(1, 1))
                c = slice((h // 2) * P, (h // 2 + 1) * P)
                product(o_bank[:, 0:N], [((v_hi[:, m, c], v_lo[:, m, c]), (pT_hi[:, m, :], pT_lo[:, m, :]))
                                         for m in range(NT)]).then_inc(o_full, 1)

            pe.wait_ge(consts_ready, 1)
            pe.wait_ge(key_ready, 1)
            for c in range((ET + 3) // 4):
                if c >= 3:
                    pe.wait_ge(key_free, c - 2)
                for j in range(min(4, ET - 4 * c)):
                    e = 4 * c + j
                    last = nc.tensor.transpose(s_bank[c % 3][:, j * P:(j + 1) * P],
                                               ekey[:, e:e + 1].to_broadcast([P, P]), ident[:, :])
                last.then_inc(key_full, 1)

            norm_T(0, 0)

            def mask_tile(slot, j, last_one=False):
                for t in range(NT):
                    last = mm(s_bank[t][:, 0:N], onehot[:, slot, j, 0, t * P:(t + 1) * P], onehot[:, slot, j, 1, :],
                              start=False, stop=last_one, skip_group_check=True)
                return last

            pe.wait_ge(key_free, (ET + 3) // 4)
            for t in range(NT):
                mm(s_bank[t][:, 0:N], zeros[:, 0:P], zeros[:, :], start=True, stop=False, skip_group_check=True)
            taken(fill_of(Index(0)))
            with pe.Fori(0, 6) as it:
                for s in range(2):
                    gemm_T(Index(U_QKV + s, it, 2), act_hi, act_lo)
                    pe.wait_ge(oh_ready, it * 2 + (s + 1))
                    for j in range(4):
                        last = mask_tile(s, j)
                    last.then_inc(oh_free, 1)
            pe.wait_ge(oh_ready, 13)
            for j in range(ET - 48):
                last = mask_tile(0, j, j == ET - 49)
            last.then_inc(mask_full, 1)

            def rest_of_group(kind, g, n, t_of, o_of, fill_tile, following=None):
                for h in range(HG):
                    def transposes(*tiles):
                        head_T(kind, g, h, lambda t: t_of(h, t), tiles)

                    def halfway():
                        if h == 3 and following:
                            following[1]()
                        transposes(2)
                        if h < 2:
                            head_scores(kind, g, h + 2)

                    transposes(0, 1)
                    if h == 3 and following:
                        following[0]()
                    fill_tile(h, halfway)
                    if h == 3 and following:
                        following[2]()
                    if h == 0:
                        taken(fill_of(n + 3))
                    head_out(h, t_of(h, 2), o_of(h))

            taken(fill_of(Index(U_QKV + 2 * GROUPS)))
            gemm_T(Index(U_GNN), act_hi, act_lo, T_K)
            gemm_T(Index(U_GNN + 1), act_hi, act_lo, T_Q)
            with pe.Fori(0, 2) as it:
                for s in range(2):
                    g = Index(s, it, 2)
                    n = Index(U_GNN + 3 * s, it, 6)

                    def next_tile(i, halfway):
                        src = (T_K, T_Q)[i // 2]
                        gemm_T(n + (3 + i // 2), act_hi, act_lo, src if s == 0 else Index(src, it, T_X - src),
                               tiles=(i % 2,), halfway=halfway)

                    taken(fill_of(n + 1) + 1)
                    pe.wait_ge(mask_ready, 2)
                    head_scores("gnn", g, 0)
                    gemm_N(n + 2, act_hi, act_lo, T_V, 0)
                    head_scores("gnn", g, 1)
                    gemm_N(n + 2, act_hi, act_lo, T_V, 1)
                    rest_of_group("gnn", g, n, lambda h, t: t_gnn(g, h, t), lambda h: pv_gnn(g, h), next_tile)

            def hidden_layer(g, m):
                pe.wait_ge(o_free, pv_hid(g, m).value(1, 1))
                product(o_bank[:, 0:N], [((w1_hi[:, :], w1_lo[:, :]), (k_hi[:, m, :], k_lo[:, m, :]))]) \
                    .then_inc(o_full, 1)

            def score_row(g):
                pe.wait_ge(o_free, pv_hid(g, 1).value(1, 2))
                pe.wait_ge(t_free, t_mix(g, 0).value(1, 1))
                for m in range(2):
                    last = mm(t_bank[0][0:HG, 0:N], w2bd[:, m, :], hid[:, m, :], start=m == 0, stop=m == 1)
                last.then_inc(t_full, 1)

            pe.wait_ge(w1_ready, 2)
            for m in range(2):
                hidden_layer(Index(0), m)
            score_row(Index(0))
            for gi in range(GROUPS):
                g = Index(gi)
                n = Index(U_MIX + 3 * gi)
                more = gi < GROUPS - 1
                taken(fill_of(n + 1) + 1)
                head_scores("mix", g, 0)

                def weights_T():
                    pe.wait_ge(row_v, g.value(3, 3))
                    pe.wait_ge(t_free, t_mix(g, 1).value(1, 1))
                    for t in range(NT):
                        last = mm(t_bank[1][:, t * HG:(t + 1) * HG], row_e[:, t * P:(t + 1) * P], ident[0:HG, 0:HG],
                                  start=True, stop=True)
                    last.then_inc(t_full, 1)

                gemm_N(n + 2, act_hi, act_lo, T_X, 0, halfway=weights_T)
                head_scores("mix", g, 1)
                gemm_N(n + 2, act_hi, act_lo, T_X, 1)

                def next_tile(i, halfway):
                    if more:
                        gemm_T(n + (3 + i // 2), act_hi, act_lo, T_X, tiles=(i % 2,), halfway=halfway)
                    else:
                        if i == 0:
                            pe.wait_ge(split_done, 1)
                        gemm_N(n + (3 + i // 2), oT_hi, oT_lo, 0, i % 2, halfway=halfway)

                rest_of_group("mix", g, n, lambda h, t: t_mix(g, 2 + 3 * h + t), lambda h: pv_mix(g, h), next_tile,
                              (lambda: (taken(fill_of(n + 4)), hidden_layer(g + 1, 0)),
                               lambda: hidden_layer(g + 1, 1), lambda: score_row(g + 1)) if more else None)

            for u in (2, 3):
                for half in range(2):
                    gemm_N(Index(U_OUT + u), oT_hi, oT_lo, 0, half)
            pe.wait_ge(split_done, 1 + GROUPS)
            with pe.Fori(0, 2) as it:
                for s in range(2):
                    for half in range(2):
                        gemm_N(Index(U_OUT + GROUPS + s, it, 2), oT_hi, oT_lo, KT, half)

            pe.wait_ge(node_ready, 1)
            pe.wait_ge(o_free, PV_NODE + 1)

            def node_scores(k):
                for a, b in ((node_hi, act_hi), (node_hi, act_lo), (node_lo, act_hi)):
                    last = mm(o_bank[0:48, 0:N], a[:, k, :], b[:, k, :], start=k == 0 and b is act_hi and a is node_hi,
                              stop=k == KT - 1 and a is node_lo)
                if k == KT - 1:
                    last.then_inc(o_full, 1)

            norm_T(1, fill_of(Index(U_FFN)).value() - LN_FILLS, node_scores)

            for f in range(3):
                def node_tiles():
                    pe.wait_ge(o_free, PV_NODE + 2)
                    for t in range(NT):
                        last = nc.tensor.transpose(o_bank[:, t * 48:(t + 1) * 48], h_tmp[0:48, t * P:(t + 1) * P],
                                                   ident[0:48, 0:48])
                    last.then_inc(o_full, 1)

                def leaf_tiles():
                    pe.wait_ge(sel_ready, 1)
                    pe.wait_ge(o_free, PV_SEL + f + 1)
                    for t in range(NT):
                        last = nc.tensor.transpose(o_bank[0:LEAVES, t * P:(t + 1) * P], sel[:, 3 * t + f, :],
                                                   ident[:, :])
                    last.then_inc(o_full, 1)

                for u in range(GROUPS):
                    n = Index(U_FFN + 8 * f + u)

                    def leaf_mask(m, out):
                        if u == 0 and m == 0:
                            pe.wait_ge(o_free, PV_SEL + f + 2)
                        cols = slice(u * MB + m * P, u * MB + (m + 1) * P)
                        return mm(out, neg_leaf[:, cols], nsel[:, :], start=False, stop=True)

                    if u:
                        gemm_T(n, act_hi, act_lo, after=leaf_mask)
                    else:
                        gemm_T(n, act_hi, act_lo, tiles=(0,), halfway=leaf_tiles, after=leaf_mask,
                               at_start=node_tiles if f == 0 else None)
                        gemm_T(n, act_hi, act_lo, tiles=(1,), after=leaf_mask)
                first = Index(U_FFN + 8 * f + 4)
                with pe.Fori(0, 2) as it:
                    for s in range(2):
                        n = first + s
                        n = Index(n.base, it, 2)
                        count = Index(4 * f + s, it, 2)

                        def bias_T(m, out):
                            if m == 0:
                                pe.wait_ge(b2_ready, count.value(1, 1))
                            c = slice(m * P, (m + 1) * P)
                            mm(out, b2_hi[s][:, c], selT[:, :], start=False, stop=False)
                            return mm(out, b2_lo[s][:, c], selT[:, :], start=False, stop=True)

                        def bias_N(t, out):
                            if t == 0:
                                pe.wait_ge(b2_ready, count.value(1, 1))
                            c = slice(t * P, (t + 1) * P)
                            mm(out, selT[:, c], b2_hi[s][:, :], start=False, stop=False)
                            return mm(out, selT[:, c], b2_lo[s][:, :], start=False, stop=True)

                        if f < 2:
                            gemm_T(n, h_hi, h_lo, after=bias_T, at_end=lambda: taken(fill_of(n)))
                        else:
                            for half in range(2):
                                gemm_N(n, h_hi, h_lo, 0, half, after=bias_N, at_end=lambda: taken(fill_of(n)))

            end = fill_of(Index(UNITS))
            for t in range(NT):
                q = S_FFN0 + t
                c = slice(t * P, (t + 1) * P)
                pe.wait_ge(e_done, q + 1)
                product(s_bank[q % 3][:, 0:N], [((qf_hi[:, k, c], qf_lo[:, k, c]), (kf_hi[:, k, :], kf_lo[:, k, :]))
                                                for k in range(KT)]).then_inc(s_full, 1)
            for t in range(NT):
                pe.wait_ge(p_ready, S_FFN0 + t + 1)
                pe.wait_ge(t_free, T_FFN0 + t + 1)
                for m in range(NT):
                    last = nc.tensor.transpose(t_bank[t % 2][:, m * P:(m + 1) * P], pf_ring[:, t, m * P:(m + 1) * P],
                                               ident[:, :])
                last.then_inc(t_full, 1)
            taken(end)
            for t in range(NT):
                c = slice(t * P, (t + 1) * P)
                pe.wait_ge(t_free, T_FFN0 + t + 3)
                for half in range(2):
                    if t:
                        pe.wait_ge(out_ready, 2 * (t - 1) + half + 1)
                    cols = slice(half * 512, (half + 1) * 512)
                    product(g_bank[half][:, :], [((pTf_hi[:, m, c], pTf_lo[:, m, c]),
                                                  (vf_hi[:, m, cols], vf_lo[:, m, cols]))
                                                 for m in range(NT)]).then_inc(g_full, 1)


def kernel(**inputs):
    import numpy as np
    import concourse.bacc as bacc
    from concourse.bass_utils import run_bass_kernel_spmd

    def arr(name):
        return np.asarray(inputs[name])

    def units(w):
        return np.ascontiguousarray(w.reshape(KT, P, GROUPS, MB).transpose(2, 1, 0, 3)).reshape(GROUPS, P, KT * MB)

    def rows(w):
        return np.ascontiguousarray(w.reshape(-1, P).T)

    def grouped(k, q, v):
        return [m[g] for g in range(GROUPS) for m in (k, q, v)]

    gnn = {k: arr("L0_gnn_" + k) for k in ("wq", "wk", "wv", "wiq", "wik", "wiv", "wo")}
    t = {k: units(w.T) for k, w in gnn.items()}
    wqkv = arr("L0_mix_Wqkv")
    mq, mk, mv_ = (units(wqkv[:, i * D:(i + 1) * D]) for i in range(3))
    first = {f: units(arr(f"L0_ffn_{f}_w1").transpose(1, 0, 2).reshape(D, D)) for f in "qkv"}
    second = {f: units(arr(f"L0_ffn_{f}_w2").reshape(D, D)) for f in "qkv"}
    stream = list(t["wq"]) + list(t["wk"]) + list(t["wv"])
    stream += grouped(t["wik"], t["wiq"], t["wiv"]) + grouped(mk, mq, mv_)
    stream += list(t["wo"]) + list(units(arr("L0_mix_Wout")))
    for f in "qkv":
        stream += list(first[f]) + list(second[f])
    wstream = np.stack(stream)
    assert wstream.shape == (UNITS, P, KT * MB)

    def wide(v):
        return np.broadcast_to(v.reshape(1, -1), (P, v.size))

    node_b = np.zeros((3, LEAVES), np.float32)
    nodes = np.zeros((3, LEAVES, D), np.float32)
    for i, f in enumerate("qkv"):
        node_b[i, :LEAVES - 1] = arr(f"L0_ffn_{f}_node_b")
        nodes[i, :LEAVES - 1] = arr(f"L0_ffn_{f}_node_w")
    pp = np.concatenate(
        [rows(arr("L0_gnn_" + b)) for b in ("bq", "bk", "bv", "biq", "bik", "biv")]
        + [rows(arr(f"L0_ffn_{f}_b1").reshape(-1)) for f in "qkv"]
        + [np.concatenate([arr("L0_mix_b1")] * 2).reshape(P, 1), wide(arr("L0_mix_b2")),
           wide(arr("L0_gnn_edge_type_weights")), wide(node_b),
           np.zeros((P, 2), np.float32)], axis=1)
    assert pp.shape == (P, PP)
    ecols = np.stack([arr(n).reshape(ET, P).T for n in ("src", "dst", "edge_type_5")], axis=1)
    consts = np.concatenate([wide(np.arange(N, dtype=np.float32)),
                             wide((2.0 ** (4.0 * (np.arange(ET) - 25))).astype(np.float32))], axis=1)
    arrays = {
        "x": arr("x"),
        "wstream": wstream,
        "ecols": ecols,
        "pp_in": pp,
        "consts": consts,
        "w1m": arr("L0_mix_W1"),
        "w2m": arr("L0_mix_W2"),
        "bo": arr("L0_gnn_bo"),
        "bout": arr("L0_mix_bout"),
        "nodes": nodes.reshape(3 * LEAVES, KT, P).transpose(2, 1, 0),
        "b2": np.stack([arr(f"L0_ffn_{f}_b2") for f in "qkv"], axis=1),
    }
    nc = bacc.Bacc("TRN2", target_bir_lowering=False, num_devices=1)
    args = {}
    for name, a in arrays.items():
        arrays[name] = a = np.ascontiguousarray(a)
        args[name] = nc.dram_tensor(f"{name}_dram", a.shape, mybir.dt.from_np(a.dtype), kind="ExternalInput").ap()
    args["out"] = nc.dram_tensor("out_dram", (N, D), F32, kind="ExternalOutput").ap()
    program(nc, **args)
    r = run_bass_kernel_spmd(nc, [{f"{k}_dram": a for k, a in arrays.items()}], core_ids=[0])
    return r.results[0]["out_dram"]
```
